# Optimizing a Trainium2 kernel written in Bass

```python
import numpy as np
import jax
import jax.numpy as jnp

def _softmax(x, axis=-1):
    return jax.nn.softmax(x, axis=axis)

def _gelu(x):
    return jax.nn.gelu(x, approximate=True)

def _silu(x):
    return jax.nn.silu(x)

def _sigmoid(x):
    return jax.nn.sigmoid(x)

def _layernorm(x, axis=-1, eps=1e-05):
    m = jnp.mean(x, axis=axis, keepdims=True)
    v = jnp.var(x, axis=axis, keepdims=True)
    return (x - m) / jnp.sqrt(v + eps)

def _scatter_add(tgt, idx, src, axis=0):
    return tgt.at[idx].add(src)

def _segment_sum(src, seg, n):
    return jax.ops.segment_sum(src, seg, n)
kernel_name = 'mk_gnn_preln_d4_gnn_r32_067235'

def setup_inputs(seed: int=0):
    np.random.seed(seed)
    _w = jnp.asarray

    def _rec_inputs():
        import jax
        import jax.numpy as jnp
        _gk = jax.random.key(seed)
        x = -0.0005121 + 1.001 * jax.random.normal(jax.random.fold_in(_gk, 1), (3125, 64), jnp.float32)
        src = jax.random.randint(jax.random.fold_in(_gk, 2), (100000,), 0, 3125, jnp.int32)
        dst = jax.random.randint(jax.random.fold_in(_gk, 3), (100000,), 0, 3125, jnp.int32)
        _o = jnp.argsort(dst, stable=True)
        src = src[_o]
        dst = dst[_o]
        edge_attr_64 = -2.25437e-05 + 0.999858 * jax.random.normal(jax.random.fold_in(_gk, 12), (100000, 64), jnp.float32)
        return (x, src, dst, edge_attr_64)
    x, src, dst, edge_attr_64 = _rec_inputs()

    def _L0_gnn_setup():
        import jax, jax.numpy as jnp
        import numpy as np
        N, E, H, D = (50000, 25000, 4, 64)
        IN = D
        EPS = 1e-05
        key = jax.random.key(seed)
        ks = jax.random.split(key, 9)
        s = 1.0 / np.sqrt(IN)
        return {'h': jax.random.normal(ks[0], (N, IN), dtype=jnp.float32), 'src': jax.random.randint(ks[1], (E,), 0, N), 'dst': jax.random.randint(ks[2], (E,), 0, N), 'Wq': jax.random.uniform(ks[3], (IN, H * D), jnp.float32, -s, s), 'Wk': jax.random.uniform(ks[4], (IN, H * D), jnp.float32, -s, s), 'Wv': jax.random.uniform(ks[5], (IN, H * D), jnp.float32, -s, s), 'Wo': jax.random.uniform(ks[6], (H * D, D), jnp.float32, -1.0 / np.sqrt(H * D), 1.0 / np.sqrt(H * D)), 'gamma': jnp.ones((D,), jnp.float32), 'beta': jnp.zeros((D,), jnp.float32)}
    _L0_gnn_all = _L0_gnn_setup()
    _L0_gnn_in = {k: v for k, v in _L0_gnn_all.items() if k in ('Wq', 'Wk', 'Wv', 'Wo', 'gamma', 'beta')}
    del _L0_gnn_all

    def _L1_gnn_setup():
        import jax, jax.numpy as jnp
        import numpy as np
        K = 3

        def _cheb_conv(x, row, col, w, W, b):
            n = x.shape[0]

            def prop(h):
                return jnp.zeros((n, h.shape[1]), h.dtype).at[row].add(w[:, None] * h[col])
            Tx0 = x
            out = Tx0 @ W[0]
            Tx1 = prop(Tx0)
            out = out + Tx1 @ W[1]
            for k in range(2, K):
                Tx2 = 2.0 * prop(Tx1) - Tx0
                out = out + Tx2 @ W[k]
                Tx0, Tx1 = (Tx1, Tx2)
            return out + b

        def _edge_norm(edge_index, n):
            row, col = (edge_index[0], edge_index[1])
            mask = (row != col).astype(jnp.float32)
            deg = jnp.zeros((n,), jnp.float32).at[row].add(mask)
            dinv = jnp.where(deg > 0, jax.lax.rsqrt(jnp.maximum(deg, 1.0)), 0.0)
            w = -dinv[row] * dinv[col] * mask
            return (row, col, w)
        key = jax.random.key(seed)
        ks = jax.random.split(key, 8)
        N, E, F_in, H = (3125, 50000, 64, 64)
        x = jax.random.normal(ks[0], (N, F_in), jnp.float32)
        edge_index = jax.random.randint(ks[1], (2, E), 0, N, jnp.int64)
        s0 = (1.0 / np.sqrt(F_in)).astype(np.float32) if isinstance(np.sqrt(F_in), np.ndarray) else np.float32(1.0 / np.sqrt(F_in))
        s1 = np.float32(1.0 / np.sqrt(H))
        W0 = jax.random.normal(ks[2], (K, F_in, H), jnp.float32) * s0
        b0 = jnp.zeros((H,), jnp.float32)
        W1 = jax.random.normal(ks[3], (K, H, H), jnp.float32) * s1
        b1 = jnp.zeros((H,), jnp.float32)
        return {'x': x, 'edge_index': edge_index, 'W0': W0, 'b0': b0, 'W1': W1, 'b1': b1}
    _L1_gnn_all = _L1_gnn_setup()
    _L1_gnn_in = {k: v for k, v in _L1_gnn_all.items() if k in ('W0', 'b0', 'W1', 'b1')}
    del _L1_gnn_all

    def _L2_gnn_setup():
        import jax, jax.numpy as jnp
        import numpy as np
        LN_EPS = 1e-05
        key = jax.random.key(seed)
        ks = jax.random.split(key, 8)
        N, E, D = (3125, 31250, 64)
        node_feats = jax.random.normal(ks[0], (N, D), dtype=jnp.float32)
        edge_feats = jax.random.normal(ks[1], (E, D), dtype=jnp.float32)
        edge_index = jax.random.randint(ks[2], (2, E), 0, N, dtype=jnp.int64)
        W1 = jax.random.normal(ks[3], (D, 2 * D), dtype=jnp.float32) / np.sqrt(D)
        b1 = jnp.zeros((2 * D,), dtype=jnp.float32)
        ln_g = jnp.ones((2 * D,), dtype=jnp.float32)
        ln_b = jnp.zeros((2 * D,), dtype=jnp.float32)
        W2 = jax.random.normal(ks[4], (2 * D, D), dtype=jnp.float32) / np.sqrt(2 * D)
        b2 = jnp.zeros((D,), dtype=jnp.float32)
        eps = jnp.zeros((1,), dtype=jnp.float32)
        return {'node_feats': node_feats, 'edge_feats': edge_feats, 'W1': W1, 'b1': b1, 'ln_g': ln_g, 'ln_b': ln_b, 'W2': W2, 'b2': b2, 'eps': eps, 'edge_index': edge_index, 'num_nodes': 3125}
    _L2_gnn_all = _L2_gnn_setup()
    _L2_gnn_in = {k: v for k, v in _L2_gnn_all.items() if k in ('W1', 'b1', 'ln_g', 'ln_b', 'W2', 'b2', 'eps')}
    del _L2_gnn_all

    def _L3_gnn_setup():
        import jax, jax.numpy as jnp
        import numpy as np
        N_NODES = 2048
        N_EDGES = 32768
        IN_DIM = 64
        OUT_DIM = 64
        key = jax.random.key(seed)
        k_h, k_src, k_dst, k_fc, k_att = jax.random.split(key, 5)
        h = jax.random.normal(k_h, (N_NODES, IN_DIM), dtype=jnp.float32)
        src_r = jax.random.randint(k_src, (N_EDGES - N_NODES,), 0, N_NODES)
        dst_r = jax.random.randint(k_dst, (N_EDGES - N_NODES,), 0, N_NODES)
        loops = jnp.arange(N_NODES)
        src = jnp.concatenate([src_r, loops]).astype(jnp.int32)
        dst = jnp.concatenate([dst_r, loops]).astype(jnp.int32)
        fc_w = jax.random.normal(k_fc, (OUT_DIM, IN_DIM), dtype=jnp.float32) * (2.0 / np.sqrt(IN_DIM + OUT_DIM))
        attn_w = jax.random.normal(k_att, (1, 2 * OUT_DIM), dtype=jnp.float32) * (2.0 / np.sqrt(2 * OUT_DIM + 1))
        return {'h': h, 'fc_w': fc_w, 'attn_w': attn_w, 'src': src, 'dst': dst}
    _L3_gnn_all = _L3_gnn_setup()
    _L3_gnn_in = {k: v for k, v in _L3_gnn_all.items() if k in ('fc_w', 'attn_w')}
    del _L3_gnn_all
    return {'x': x, 'src': src, 'dst': dst, 'edge_attr_64': edge_attr_64, 'L0_gnn_Wq': _L0_gnn_in['Wq'], 'L0_gnn_Wk': _L0_gnn_in['Wk'], 'L0_gnn_Wv': _L0_gnn_in['Wv'], 'L0_gnn_Wo': _L0_gnn_in['Wo'], 'L0_gnn_gamma': _L0_gnn_in['gamma'], 'L0_gnn_beta': _L0_gnn_in['beta'], 'L1_gnn_W0': _L1_gnn_in['W0'], 'L1_gnn_b0': _L1_gnn_in['b0'], 'L1_gnn_W1': _L1_gnn_in['W1'], 'L1_gnn_b1': _L1_gnn_in['b1'], 'L2_gnn_W1': _L2_gnn_in['W1'], 'L2_gnn_b1': _L2_gnn_in['b1'], 'L2_gnn_ln_g': _L2_gnn_in['ln_g'], 'L2_gnn_ln_b': _L2_gnn_in['ln_b'], 'L2_gnn_W2': _L2_gnn_in['W2'], 'L2_gnn_b2': _L2_gnn_in['b2'], 'L2_gnn_eps': _L2_gnn_in['eps'], 'L3_gnn_fc_w': _L3_gnn_in['fc_w'], 'L3_gnn_attn_w': _L3_gnn_in['attn_w']}

def reference(x, src, dst, edge_attr_64, L0_gnn_Wq, L0_gnn_Wk, L0_gnn_Wv, L0_gnn_Wo, L0_gnn_gamma, L0_gnn_beta, L1_gnn_W0, L1_gnn_b0, L1_gnn_W1, L1_gnn_b1, L2_gnn_W1, L2_gnn_b1, L2_gnn_ln_g, L2_gnn_ln_b, L2_gnn_W2, L2_gnn_b2, L2_gnn_eps, L3_gnn_fc_w, L3_gnn_attn_w):
    import jax
    import jax.numpy as jnp

    def _L0_gnn_ref(h, src, dst, Wq, Wk, Wv, Wo, gamma, beta):
        import jax, jax.numpy as jnp
        import numpy as np
        N, E, H, D = (50000, 25000, 4, 64)
        IN = D
        EPS = 1e-05
        n = h.shape[0]
        Q = (h @ Wq).reshape(n, H, D)
        K = (h @ Wk).reshape(n, H, D)
        V = (h @ Wv).reshape(n, H, D)
        score = jnp.einsum('ehd,ehd->eh', Q[src], K[dst]) / np.sqrt(D)
        attn = jax.nn.softmax(score, axis=1)
        m = V[src] * attn[:, :, None]
        h_new = jax.ops.segment_sum(m, dst, num_segments=n)
        h_proj = h_new.reshape(n, H * D) @ Wo
        x = h_proj + h
        mu = jnp.mean(x, axis=-1, keepdims=True)
        var = jnp.mean((x - mu) ** 2, axis=-1, keepdims=True)
        return (x - mu) * jax.lax.rsqrt(var + EPS) * gamma + beta

    def _L1_gnn_ref(x, edge_index, W0, b0, W1, b1):
        import jax, jax.numpy as jnp
        import numpy as np
        K = 3

        def _cheb_conv(x, row, col, w, W, b):
            n = x.shape[0]

            def prop(h):
                return jnp.zeros((n, h.shape[1]), h.dtype).at[row].add(w[:, None] * h[col])
            Tx0 = x
            out = Tx0 @ W[0]
            Tx1 = prop(Tx0)
            out = out + Tx1 @ W[1]
            for k in range(2, K):
                Tx2 = 2.0 * prop(Tx1) - Tx0
                out = out + Tx2 @ W[k]
                Tx0, Tx1 = (Tx1, Tx2)
            return out + b

        def _edge_norm(edge_index, n):
            row, col = (edge_index[0], edge_index[1])
            mask = (row != col).astype(jnp.float32)
            deg = jnp.zeros((n,), jnp.float32).at[row].add(mask)
            dinv = jnp.where(deg > 0, jax.lax.rsqrt(jnp.maximum(deg, 1.0)), 0.0)
            w = -dinv[row] * dinv[col] * mask
            return (row, col, w)
        n = x.shape[0]
        row, col, w = _edge_norm(edge_index, n)
        h = jax.nn.relu(_cheb_conv(x, row, col, w, W0, b0))
        h = jax.nn.relu(_cheb_conv(h, row, col, w, W1, b1))
        return h

    def _L2_gnn_ref(node_feats, edge_feats, W1, b1, ln_g, ln_b, W2, b2, eps, edge_index, num_nodes):
        import jax, jax.numpy as jnp
        import numpy as np
        LN_EPS = 1e-05
        message = jax.nn.relu(node_feats[edge_index[1]] + edge_feats)
        message_reduce = jax.ops.segment_sum(message, edge_index[0], num_segments=num_nodes)
        h = (1.0 + eps) * node_feats + message_reduce
        x = h @ W1 + b1
        mu = jnp.mean(x, axis=-1, keepdims=True)
        var = jnp.mean(jnp.square(x - mu), axis=-1, keepdims=True)
        x = (x - mu) * jax.lax.rsqrt(var + LN_EPS) * ln_g + ln_b
        x = jax.nn.relu(x)
        return x @ W2 + b2

    def _L3_gnn_ref(h, fc_w, attn_w, src, dst):
        import jax, jax.numpy as jnp
        import numpy as np
        N_NODES = 2048
        N_EDGES = 32768
        IN_DIM = 64
        OUT_DIM = 64
        'GAT_Layer.forward (dropout=0): z = fc(h); per-edge e = leaky_relu(attn([z_src||z_dst]));\n            softmax over incoming edges of each dst node; h_out = sum alpha * z_src.'
        n = h.shape[0]
        z = h @ fc_w.T
        a_src = attn_w[0, :OUT_DIM]
        a_dst = attn_w[0, OUT_DIM:]
        es = z @ a_src
        ed = z @ a_dst
        e = jax.nn.leaky_relu(es[src] + ed[dst], negative_slope=0.01)
        emax = jnp.full((n,), -jnp.inf, dtype=e.dtype).at[dst].max(e)
        emax = jnp.where(jnp.isfinite(emax), emax, 0.0)
        w = jnp.exp(e - emax[dst])
        denom = jnp.zeros((n,), dtype=e.dtype).at[dst].add(w)
        denom = jnp.where(denom > 0, denom, 1.0)
        alpha = w / denom[dst]
        h_out = jnp.zeros((n, z.shape[1]), dtype=z.dtype).at[dst].add(alpha[:, None] * z[src])
        return h_out
    edge_index = jnp.stack([src, dst])
    h = jnp.maximum(_layernorm(x, axis=-1), 0.0)
    x = x + _L0_gnn_ref(h, src, dst, L0_gnn_Wq, L0_gnn_Wk, L0_gnn_Wv, L0_gnn_Wo, L0_gnn_gamma, L0_gnn_beta)
    h = jnp.maximum(_layernorm(x, axis=-1), 0.0)
    x = x + _L1_gnn_ref(h, edge_index, L1_gnn_W0, L1_gnn_b0, L1_gnn_W1, L1_gnn_b1)
    h = jnp.maximum(_layernorm(x, axis=-1), 0.0)
    x = x + _L2_gnn_ref(h, edge_attr_64, L2_gnn_W1, L2_gnn_b1, L2_gnn_ln_g, L2_gnn_ln_b, L2_gnn_W2, L2_gnn_b2, L2_gnn_eps, edge_index, 3125)
    h = jnp.maximum(_layernorm(x, axis=-1), 0.0)
    x = x + _L3_gnn_ref(h, L3_gnn_fc_w, L3_gnn_attn_w, src, dst)
    return x

_drawn_inputs = setup_inputs


def setup_inputs(seed=0):
    import zlib

    import numpy as np

    out = dict(_drawn_inputs(seed))
    spreads = {'L0_gnn_gamma': (1.0, 0.2),
     'L0_gnn_beta': (0.0, 0.1),
     'L1_gnn_b0': (0.0, 0.1),
     'L1_gnn_b1': (0.0, 0.1),
     'L2_gnn_b1': (0.0, 0.8),
     'L2_gnn_ln_g': (1.0, 0.2),
     'L2_gnn_ln_b': (0.0, 0.275),
     'L2_gnn_b2': (0.0, 0.1)}
    factors = {}
    for name, (base, spread) in spreads.items():
        noise = np.random.default_rng([zlib.crc32(name.encode()), seed]).standard_normal(out[name].shape)
        drawn = base * np.exp(spread * noise) if base else spread * noise
        out[name] = jnp.asarray(drawn.astype(out[name].dtype))
    for name, factor in factors.items():
        out[name] = (out[name] * factor).astype(out[name].dtype)
    return out
```

```python
from contextlib import ExitStack

import numpy as np

import concourse.bass as bass
import concourse.mybir as mybir

F32 = mybir.dt.float32
BF16 = mybir.dt.bfloat16
I32 = mybir.dt.int32
I16 = mybir.dt.int16
ALU = mybir.AluOpType
ACT = mybir.ActivationFunctionType
AX = mybir.AxisListType

P = 128
N = 3125
D = 64
E = 100000
H = 4
NB = -(-N // P)
NP = NB * P
LAST = N - (NB - 1) * P
TP = 125
T = 8
GE = TP * T
G = E // GE
W = 40
NPW = NP + W
SP3 = 3
KW = SP3 * W
KEYS = NB * W
MAXWIN = -(-N // W)
IC = 62
assert P * IC > G * MAXWIN and G * GE == E and KEYS <= 1024
EPS = 1e-5
FAR = 8192.0
NACC = 4
ACCR = NP + P


class Shared:
    pass


class Own:

    def __init__(self, eng, sem, base=0):
        self.eng, self.sem, self.base, self.n = eng, sem, base, 0

    def did(self, ins):
        ins.then_inc(self.sem, 1)
        self.n += 1
        return self.n

    def settle(self, step=None):
        self.eng.wait_ge(self.sem, self.base + (step or self.n))

    def step(self, ins):
        self.did(ins)
        self.settle()


def over(ap, shape):
    return ap.unsqueeze(2).to_broadcast(shape)


def norm_steps(nc, own, src, out, tmp, st, width, relu, act_turn):
    b = src.shape[1]
    full = [P, b, width]
    own.step(nc.vector.tensor_reduce(st[:, 0, 0:b], src, AX.X, ALU.add))
    own.step(nc.vector.tensor_scalar(st[:, 1, 0:b], st[:, 0, 0:b], 1.0 / width, None, ALU.mult))
    own.step(nc.vector.tensor_tensor(out, src, over(st[:, 1, 0:b], full), ALU.subtract))
    own.step(nc.vector.tensor_tensor(tmp, out, out, ALU.mult))
    own.step(nc.vector.tensor_reduce(st[:, 0, 0:b], tmp, AX.X, ALU.add))
    own.step(nc.vector.tensor_scalar(st[:, 1, 0:b], st[:, 0, 0:b], 1.0 / width, EPS, ALU.mult, ALU.add))
    own.step(nc.vector.reciprocal(st[:, 2, 0:b], st[:, 1, 0:b]))
    act_turn()
    own.step(nc.vector.tensor_tensor(tmp, out, over(st[:, 3, 0:b], full), ALU.mult))
    if relu:
        own.step(nc.vector.tensor_scalar(out, tmp, 0.0, None, ALU.max))


def root(nc, st, b):
    return nc.scalar.activation(st[:, 3, 0:b], st[:, 2, 0:b], ACT.Sqrt)


def prepare(nc, I, S, sb, sem):
    B = S.A
    at = [0]

    def carve(cols, dt=F32):
        v = B[:, at[0]:at[0] + 2 * cols] if dt != BF16 else B[:, at[0]:at[0] + cols]
        at[0] += 2 * cols if dt != BF16 else cols
        return v if dt == BF16 else v.bitcast(dt)

    X = carve(NB * D).rearrange("p (b f) -> p b f", b=NB)
    Hn = carve(NB * D).rearrange("p (b f) -> p b f", b=NB)
    tmp = carve(NB * D).rearrange("p (b f) -> p b f", b=NB)
    st = carve(4 * NB).rearrange("p (s b) -> p s b", s=4)
    srcI, dstI, shI = carve(G * T, I32), carve(G * T, I32), carve(G * T, I32)
    dg = carve(GE, I32)
    ramp = carve(KEYS, I32)
    ibase = carve(IC, I32)
    tri, shift = carve(P), carve(P)
    w40 = carve(MAXWIN, I32)
    gm = carve(16)
    nwB, dB = carve(P), carve(P)
    ends, jumps = carve(P), carve(P)
    past = carve(IC * G).rearrange("p (c g) -> p c g", c=IC)
    moved = past
    reach = past[:, 0, :]
    gi, bi, ifl = carve(IC), carve(IC), carve(IC)
    item = carve(IC * 2, I32).rearrange("p (c k) -> p c k", k=2)
    Wt = carve(3 * H * D).rearrange("p (w c) -> p w c", w=3)
    Wo = carve(H * D).rearrange("p (h o) -> p h o", h=H)
    WT = carve(3 * H * D).rearrange("p (w c) -> p w c", w=3)
    Mk = carve(H * D)
    HT = carve(NP)
    R3 = carve(NB * SP3 * H * D, BF16).rearrange("p (b s c) -> p b s c", b=NB, s=SP3)
    rest = carve(2 * 2 * 512).rearrange("p (r c) -> p r c", r=4)
    zero = carve(SP3 * H * D, BF16)
    edges = carve(G * 3 * T).rearrange("p (g k t) -> p g k t", g=G, k=3)
    assert at[0] <= NB * NP

    q = {n: sem("p_" + n) for n in (
        "x", "src", "dst", "dgrp", "w", "const", "own", "ownp", "var", "root", "wdone", "wtp", "wt", "mk", "mkc",
        "tile", "nw", "cum", "items", "h", "htp", "ht", "r", "hi", "rem", "mid", "lo", "stored", "pads", "edges")}

    with nc.Block() as block:

        @block.sync
        def _(sp):
            sp.wait_ge(q["pads"], 3)
            sp.dma_start(X[:, 0:NB - 1, :], I["x"][0:(NB - 1) * P, :].rearrange("(b p) f -> p b f", p=P)).then_inc(q["x"], 16)
            sp.dma_start(X[0:LAST, NB - 1, :], I["x"][(NB - 1) * P:N, :]).then_inc(q["x"], 16)
            sp.dma_start(dg[0:G, :], I["dst"].rearrange("(g e) -> g e", g=G)).then_inc(q["dgrp"], 16)
            sp.dma_start(srcI[0:TP, :].rearrange("p (g t) -> p g t", t=T),
                         I["src"].rearrange("(g p t) -> p g t", p=TP, t=T)).then_inc(q["src"], 16)
            sp.dma_start(dstI[0:TP, :].rearrange("p (g t) -> p g t", t=T),
                         I["dst"].rearrange("(g p t) -> p g t", p=TP, t=T)).then_inc(q["dst"], 16)
            for k, w in enumerate((I["L0_gnn_Wq"], I["L0_gnn_Wk"], I["L0_gnn_Wv"])):
                sp.dma_start(Wt[0:D, k, :], w).then_inc(q["w"], 16)
            sp.dma_start(Wo[0:D, :, :], I["L0_gnn_Wo"].rearrange("(h c) o -> c h o", h=H)).then_inc(q["w"], 16)
            sp.wait_ge(q["items"], 1)
            sp.dma_start(S.items.rearrange("(p c) k -> p (c k)", p=P), item.rearrange("p c k -> p (c k)")).then_inc(q["stored"], 16)
            sp.wait_ge(q["h"], 1)
            sp.dma_start(S.h0.rearrange("(b p) f -> p b f", p=P), Hn).then_inc(q["stored"], 16)
            sp.dma_start(S.r3[NP:NPW].rearrange("n s c -> n (s c)"), zero[0:W, :]).then_inc(q["stored"], 16)
            sp.wait_ge(q["lo"], NB)
            sp.dma_start(S.r3[0:NP].rearrange("(b p) s c -> p b (s c)", p=P), R3.rearrange("p b s c -> p b (s c)")).then_inc(q["stored"], 16)
            sp.wait_ge(q["edges"], 1)
            sp.dma_start(S.edges.rearrange("g p k t -> p g (k t)"), edges[0:TP].rearrange("p g k t -> p g (k t)")).then_inc(q["stored"], 16)
            sp.wait_ge(q["stored"], 80)

        @block.gpsimd
        def _(g):
            own = Own(g, q["ownp"])
            own.did(g.memset(S.ident[:, :], 0.0))
            own.did(g.memset(tri, 1.0))
            own.did(g.memset(shift, 0.0))
            g.iota(ramp, pattern=[[1, KEYS]], base=0, channel_multiplier=0).then_inc(q["const"], 1)
            g.iota(ibase, pattern=[[1, IC]], base=0, channel_multiplier=IC).then_inc(q["const"], 1)
            g.iota(w40, pattern=[[W, MAXWIN]], base=W, channel_multiplier=0).then_inc(q["const"], 1)
            g.iota(S.third[:, :], pattern=[[0, 1]], base=0, channel_multiplier=171).then_inc(q["const"], 1)
            own.settle()
            g.affine_select(out=S.ident[:, :], in_=S.ident[:, :], compare_op=ALU.not_equal, fill=1.0, base=0,
                            pattern=[[-1, P]], channel_multiplier=1).then_inc(q["const"], 1)
            g.affine_select(out=tri, in_=tri, compare_op=ALU.is_ge, fill=0.0, base=0,
                            pattern=[[1, P]], channel_multiplier=-1).then_inc(q["const"], 1)
            own.step(g.affine_select(out=shift, in_=shift, compare_op=ALU.not_equal, fill=1.0, base=-1,
                                     pattern=[[-1, P]], channel_multiplier=1))
            own.step(g.affine_select(out=shift, in_=shift, compare_op=ALU.not_equal, fill=-1.0, base=0,
                                     pattern=[[-1, P]], channel_multiplier=1))
            g.memset(shift[:, G:G + 1], 0.0).then_inc(q["ownp"], 1)
            g.wait_ge(q["ownp"], 6)
            g.memset(shift[0:1, G:G + 1], 1.0).then_inc(q["const"], 1)

        @block.vector
        def _(v):
            own = Own(v, q["own"])
            v.memset(X[:, NB - 1, :], 0.0).then_inc(q["pads"], 1)
            v.memset(srcI, 0.0).then_inc(q["pads"], 1)
            v.memset(dstI, -4096.0).then_inc(q["pads"], 1)
            own.did(v.memset(zero, 0.0))
            own.did(v.memset(S.hpT[:, :], 0.0))
            v.wait_ge(q["const"], 7)
            own.did(v.tensor_copy(S.ramp[:, :], ramp))
            own.did(v.tensor_copy(S.identb[:, :], S.ident[:, :]))
            own.step(v.tensor_scalar(S.third[:, :], S.third[:, :], 9, None, ALU.logical_shift_right))
            own.did(v.tensor_copy(S.thirdf[:, :], S.third[:, :]))
            v.wait_ge(q["dgrp"], 16)
            own.did(v.tensor_reduce(gm[0:G, 0:1], dg[0:G, :], AX.X, ALU.max))
            own.step(v.tensor_reduce(gm[0:G, 1:2], dg[0:G, :], AX.X, ALU.min))
            own.step(v.tensor_tensor(gm[0:G, 2:3], gm[0:G, 0:1], gm[0:G, 1:2], ALU.subtract))
            own.step(v.tensor_scalar(reach[0:G, 0:MAXWIN], w40[0:G, :], gm[0:G, 2:3], None, ALU.is_le))
            own.step(v.tensor_reduce(gm[0:G, 3:4], reach[0:G, 0:MAXWIN], AX.X, ALU.add))
            own.step(v.tensor_scalar(gm[0:G, 4:5], gm[0:G, 3:4], 1.0, None, ALU.add))
            v.tensor_copy(nwB[0:G, :], gm[0:G, 4:5].to_broadcast([G, P])).then_inc(q["nw"], 1)
            v.wait_ge(q["cum"], 1)
            own.step(v.tensor_tensor(gm[0:G, 5:6], S.bank[1][0:G, 0:1], gm[0:G, 4:5], ALU.subtract))
            own.step(v.scalar_tensor_tensor(gm[0:G, 6:7], gm[0:G, 5:6], -float(W), gm[0:G, 1:2], ALU.mult, ALU.add))
            v.tensor_copy(dB[0:G, :], gm[0:G, 6:7].to_broadcast([G, P])).then_inc(q["nw"], 1)
            own.did(v.tensor_copy(ends[:, 0:G], S.bank[0][:, 0:G]))
            v.wait_ge(q["cum"], 2)
            own.step(v.tensor_copy(jumps[:, 0:G + 1], S.bank[2][:, 0:G + 1]))
            own.did(v.tensor_copy(S.count[:, 0:1], ends[0:1, G - 1:G]))
            own.step(v.scalar_tensor_tensor(jumps[:, G - 1:G], ends[:, G - 1:G], -float(W), jumps[:, G - 1:G], ALU.mult, ALU.add))
            own.step(v.tensor_scalar(jumps[:, G - 1:G], jumps[:, G - 1:G], float(NP - W), None, ALU.add))
            own.step(v.tensor_scalar(S.count[:, 2:3], S.count[:, 0:1], 1.0, None, ALU.add))
            own.step(v.tensor_scalar(S.count[:, 1:2], S.count[:, 2:3], 1, None, ALU.logical_shift_right))
            full = [P, IC, G]
            own.step(v.tensor_copy(ifl, ibase))
            own.step(v.tensor_tensor(past, over(ifl, full), ends[:, 0:G].unsqueeze(1).to_broadcast(full), ALU.is_ge))
            own.step(v.tensor_reduce(gi, past, AX.X, ALU.add))
            own.step(v.tensor_tensor(moved, past, jumps[:, 0:G].unsqueeze(1).to_broadcast(full), ALU.mult))
            own.step(v.tensor_reduce(bi, moved, AX.X, ALU.add))
            own.did(v.tensor_scalar(item[:, :, 0], gi, float(G - 1), None, ALU.min))
            own.step(v.tensor_scalar(bi, bi, jumps[:, G:G + 1], None, ALU.add))
            v.scalar_tensor_tensor(item[:, :, 1], ifl, float(W), bi, ALU.mult, ALU.add).then_inc(q["items"], 1)
            v.wait_ge(q["x"], 32)

            def act_turn():
                v.sem_inc(q["var"], 1)
                v.wait_ge(q["root"], 1)

            norm_steps(nc, own, X, Hn, tmp, st, D, True, act_turn)
            v.sem_inc(q["h"], 1)
            v.wait_ge(q["src"], 16)
            v.wait_ge(q["dst"], 16)
            own.step(v.tensor_scalar(shI, srcI, 7, None, ALU.arith_shift_right))
            own.did(v.tensor_copy(edges[:, :, 1, :], shI.rearrange("p (g t) -> p g t", t=T)))
            own.step(v.tensor_scalar(srcI, srcI, P - 1, None, ALU.bitwise_and))
            own.did(v.tensor_copy(edges[:, :, 2, :], srcI.rearrange("p (g t) -> p g t", t=T)))
            own.step(v.tensor_copy(edges[:, :, 0, :], dstI.rearrange("p (g t) -> p g t", t=T)))
            v.sem_inc(q["edges"], 1)
            for b in range(NB):
                r = S.bank[4 + b % 4][:, 0:H * D]
                v.wait_ge(q["hi"], b + 1)
                v.tensor_tensor(rest[:, b % 4, 0:H * D], r, R3[:, b, 0, :], ALU.subtract).then_inc(q["rem"], 1)
                v.wait_ge(q["mid"], b + 1)
                v.tensor_tensor(R3[:, b, 2, :], rest[:, b % 4, 0:H * D], R3[:, b, 1, :], ALU.subtract).then_inc(q["lo"], 1)

        @block.scalar
        def _(act):
            act.wait_ge(q["var"], 1)
            root(nc, st, NB).then_inc(q["root"], 1)
            for k in range(3):
                act.wait_ge(q["wtp"], k + 1)
                nc.scalar.activation(WT[0:D, k, :], S.bank[(3, 5, 6)[k]][0:D, 0:H * D],
                                     ACT.Copy, scale=D ** -0.5 if k == 0 else 1.0).then_inc(q["wt"], 1)
            act.wait_ge(q["mk"], 1)
            act.copy(Mk[0:D, :], S.bank[7][0:D, 0:H * D]).then_inc(q["mkc"], 1)
            act.copy(S.Mo[:, :], S.bank[4][0:D, 0:H * D]).then_inc(q["mkc"], 1)
            for b in range(NB + 1):
                if b < NB:
                    act.wait_ge(q["htp"], b + 1)
                    act.copy(HT[0:D, b * P:(b + 1) * P], S.bank[1 + b % 2][0:D, 0:P]).then_inc(q["ht"], 1)
                if b >= 1:
                    c = b - 1
                    act.wait_ge(q["r"], c + 1)
                    act.copy(R3[:, c, 0, :], S.bank[4 + c % 4][:, 0:H * D]).then_inc(q["hi"], 1)
                    act.wait_ge(q["rem"], c + 1)
                    act.copy(R3[:, c, 1, :], rest[:, c % 4, 0:H * D]).then_inc(q["mid"], 1)

        @block.tensor
        def _(pe):
            pe.wait_ge(q["const"], 7)
            pe.wait_ge(q["nw"], 1)
            pe.matmul(S.bank[0][:, 0:G], nwB[0:G, :], tri[0:G, 0:G], start=True, stop=True)
            pe.matmul(S.bank[1][0:G, 0:1], tri[0:G, 0:G], nwB[0:G, 0:1], start=True, stop=True).then_inc(q["cum"], 1)
            pe.wait_ge(q["nw"], 2)
            pe.matmul(S.bank[2][:, 0:G + 1], dB[0:G, :], shift[0:G, 0:G + 1], start=True, stop=True).then_inc(q["cum"], 1)
            pe.wait_ge(q["w"], 64)
            for k in range(3):
                o = S.bank[(3, 5, 6)[k]][0:D, 0:H * D]
                for h in range(H):
                    mm = pe.transpose(o[:, h * D:(h + 1) * D], Wt[0:D, k, h * D:(h + 1) * D], S.ident[0:D, 0:D])
                mm.then_inc(q["wtp"], 1)
            pe.wait_ge(q["wt"], 3)
            for h in range(H):
                c = slice(h * D, (h + 1) * D)
                pe.matmul(S.bank[7][0:D, c], WT[0:D, 1, c], WT[0:D, 0, c], start=True, stop=True)
                mm = pe.matmul(S.bank[4][0:D, c], WT[0:D, 2, c], Wo[0:D, h, :], start=True, stop=True)
            mm.then_inc(q["mk"], 1)
            pe.wait_ge(q["mkc"], 2)
            pe.wait_ge(q["h"], 1)
            for b in range(NB + 1):
                if b < NB:
                    if b >= 2:
                        pe.wait_ge(q["ht"], b - 1)
                    pe.transpose(S.bank[1 + b % 2][0:D, 0:P], Hn[:, b, :], S.ident[:, :]).then_inc(q["htp"], 1)
                if b >= 1:
                    c = b - 1
                    pe.wait_ge(q["ht"], c + 1)
                    if c >= 4:
                        pe.wait_ge(q["rem"], c - 3)
                    pe.matmul(S.bank[4 + c % 4][:, 0:H * D], HT[0:D, c * P:(c + 1) * P], Mk[0:D, :],
                              start=True, stop=True).then_inc(q["r"], 1)


def attend(nc, I, S, sb, sem):
    HT = T // 2
    spot = sb("spot", [P, 2, 2], I32)
    idx = sb("idx", [P, 2, T], I32)
    dstrow = sb("dstrow", [KW, GE], I32)
    rwin = sb("rwin", [KW, 2, H * D], BF16)
    hsrc = sb("hsrc", [P, 2, T, D], F32)
    there = sb("there", [KW, 2, GE], BF16)
    lo = sb("lo", [P, T, P], BF16)
    hot = sb("hot", [P, 2, KEYS], BF16)
    prod = sb("prod", [P, HT * H * D], F32)
    at = sb("at", [P, T, W], BF16)
    AO = sb("AO", [P, 2, HT, H, W], F32)
    edges = sb("edges", [P, 2, 3, T], F32)
    small = sb("small", [P, 6, T * H], F32)
    last = sb("last", [1, 1], I32)
    thr = sb("thr", [P, 1], F32)
    U = sb("U", [D, H * W], F32)
    dl, key, top = (small[0:TP, k, 0:T] for k in range(3))
    score, expo, attn = (small[0:TP, k, :] for k in range(3, 6))

    q = {n: sem("a_" + n) for n in (
        "spot0", "spot1", "edges0", "edges1", "idx0", "idx1", "rwin0", "rwin1", "dstrow", "zero", "pad", "spot_free", "window_free", 
        "there", "lo", "lo_free", "hot", "hot_free", "scores", "scores_free", "soft", "expo", "ao", "ao_free", "carrier",
        "idx_free", "counted", "count_free", "u", "u_free", "u_zero", "ucopy", "proj", "proj_free", "own")}
    got = [[sem(f"a_got{s}{t}") for t in range(T)] for s in range(2)]
    STEPS = 10
    half = NB * NP // 2

    def pairs_of(eng):
        return eng.value_load(S.count[0:1, 1:2], min_val=1, max_val=P * IC // 2)

    with nc.Block() as block:

        @block.sync
        def _(sp):
            sp.wait_ge(q["pad"], 1)
            with sp.Fori(0, pairs_of(sp)) as j:
                for s in range(2):
                    i = j * 2 + s
                    g = sp.value_load(S.items[bass.ds(i, 1), 0:1], min_val=0, max_val=G - 1)
                    b = sp.value_load(S.items[bass.ds(i, 1), 1:2], min_val=0, max_val=NP - W)
                    sp.wait_ge(q["spot_free"], i + 1)
                    sp.dma_start(spot[:, s, :], S.items[bass.ds(i, 1), :].to_broadcast([P, 2])).then_inc(q[f"spot{s}"], 16)
                    sp.dma_start(edges[0:TP, s, :, :], S.edges[bass.ds(g, 1)].rearrange("g p k t -> p (g k) t")).then_inc(q[f"edges{s}"], 16)
                    sp.wait_ge(q["idx_free"], i + 1)
                    sp.dma_start(idx[0:TP, s, :], I["src"][bass.ds(g * GE, GE)].rearrange("(p t) -> p t", t=T)).then_inc(q[f"idx{s}"], 16)
                    sp.wait_ge(q["window_free"], i + 1)
                    sp.dma_start(rwin[:, s, :], S.r3[bass.ds(b, W)].rearrange("n s c -> (n s) c")).then_inc(q[f"rwin{s}"], 16)
                    sp.wait_ge(q["there"], i + 1)
                    sp.dma_start(dstrow[:, :], I["dst"][bass.ds(g * GE, GE)].unsqueeze(0).to_broadcast([KW, GE])).then_inc(q["dstrow"], 16)

        @block.gpsimd
        def _(g):
            g.memset(idx[:, :, :], 0.0).then_inc(q["pad"], 1)
            g.memset(U[:, :], 0.0).then_inc(q["u_zero"], 1)
            g.memset(S.A[:, half:2 * half].bitcast(F32), 0.0).then_inc(q["zero"], 1)
            with g.Fori(0, pairs_of(g)) as j:
                for s in range(2):
                    i = j * 2 + s
                    g.wait_ge(q[f"idx{s}"], j * 16 + 16)
                    g.wait_ge(q["ao_free"], 2 * i + 2)
                    g.sem_inc(q["carrier"], 1)
                    for t in range(T):
                        g.indirect_dma_start(out=hsrc[:, s, t, :], out_offset=None, in_=S.h0[:, :],
                                             in_offset=bass.IndirectOffsetOnAxis(ap=idx[:, s, t:t + 1], axis=0)
                                             ).then_inc(got[s][t], 16)

        @block.vector
        def _(v):
            v.sem_inc(q["spot_free"], 2)
            v.sem_inc(q["there"], 1)
            v.sem_inc(q["scores_free"], 2)
            v.sem_inc(q["proj_free"], 1)
            v.sem_inc(q["count_free"], 2)
            v.sem_inc(q["idx_free"], 2)
            first = Own(v, q["own"])
            first.step(v.memset(last[:, :], 0.0))
            v.memset(S.A[:, 0:half].bitcast(F32), 0.0).then_inc(q["zero"], 1)
            v.wait_ge(q["zero"], 2)
            with v.Fori(0, pairs_of(v)) as j:
                for s in range(2):
                    i = j * 2 + s
                    own = Own(v, q["own"], j * (2 * STEPS + 1) + s * STEPS + 1)
                    th = "p (t h) -> p t h"
                    four = [TP, HT, H, D]
                    s4, e4, a4 = (x.rearrange(th, h=H) for x in (score, expo, attn))

                    def keys(t0, t1):
                        for t in range(t0, t1):
                            v.wait_ge(q["hot_free"], T * i + t + 1)
                            v.tensor_scalar(hot[0:TP, t % 2, :], S.ramp[0:TP, :], key[:, t:t + 1], None,
                                            ALU.is_equal).then_inc(q["hot"], 1)

                    def products(hf):
                        v.wait_ge(q["scores"], 2 * i + hf + 1)
                        for t in range(HT):
                            v.wait_ge(got[s][HT * hf + t], j * 16 + 16)
                        v.tensor_tensor(prod[0:TP, :].rearrange("p (t h f) -> p t h f", t=HT, h=H),
                                        S.ps[0:TP, hf * 1024:(hf + 1) * 1024].rearrange("p (t h f) -> p t h f", t=HT, h=H),
                                        hsrc[0:TP, s, HT * hf:HT * (hf + 1), :].unsqueeze(2).to_broadcast(four),
                                        ALU.mult).then_inc(q["scores_free"], 1)

                    def sums(hf):
                        v.wait_ge(q["scores_free"], 2 * i + hf + 3)
                        return own.did(v.tensor_reduce(score[:, hf * HT * H:(hf + 1) * HT * H],
                                                       prod[0:TP, :].rearrange("p (c f) -> p c f", f=D), AX.X, ALU.add))

                    def add_counts(k):
                        part = S.A[:, :].rearrange("p (b n) -> p b n", b=NB)[:, :, bass.ds(b + k * (W // 2), W // 2)]
                        seen = S.ps[:, 2048 + 512 * k:2048 + 512 * k + KEYS // 2].rearrange("p (w b) -> p b w", b=NB)
                        v.tensor_tensor(part, part, seen, ALU.add).then_inc(q["count_free"], 1)

                    v.wait_ge(q[f"spot{s}"], j * 16 + 16)
                    own.did(v.tensor_scalar(thr[0:KW, :], S.thirdf[0:KW, :], spot[0:KW, s, 1:2], None, ALU.add))
                    v.wait_ge(q[f"edges{s}"], j * 16 + 16)
                    placed = own.did(v.tensor_scalar(dl, edges[0:TP, s, 0, :], spot[0:TP, s, 1:2], None, ALU.subtract))
                    b = v.value_load(spot[0:1, s, 1:2], min_val=0, max_val=NP - W)
                    if s == 0:
                        before, b0 = v.value_load(last[0:1, 0:1], min_val=0, max_val=NP - W), b
                    else:
                        before = b0
                        own.did(v.tensor_copy(last[:, :], spot[0:1, s, 1:2]))
                    v.wait_ge(q["window_free"], i + 1)
                    v.wait_ge(q["dstrow"], i * 16 + 16)
                    own.settle(placed)
                    v.tensor_scalar(there[:, s, :], dstrow[:, :], thr[0:KW, :], None, ALU.is_equal).then_inc(q["there"], 1)
                    keyed = own.did(v.scalar_tensor_tensor(key, dl, float(NB), edges[0:TP, s, 1, :], ALU.mult, ALU.add))
                    v.wait_ge(q["lo_free"], i + 1)
                    for t in range(T):
                        op = v.tensor_scalar(lo[0:TP, t, :], S.ramp[0:TP, 0:P], edges[0:TP, s, 2, t:t + 1], None, ALU.is_equal)
                    op.then_inc(q["lo"], 1)
                    own.settle(keyed)
                    keys(0, 2)
                    products(0)
                    keys(2, 4)
                    sums(0)
                    keys(4, 6)
                    own.settle()
                    products(1)
                    v.sem_inc(q["idx_free"], 1)
                    keys(6, 8)
                    summed = sums(1)
                    own.did(v.tensor_tensor(at[0:TP, :, :], S.ramp[0:TP, 0:W].unsqueeze(1).to_broadcast([TP, T, W]),
                                            over(dl, [TP, T, W]), ALU.is_equal))
                    v.sem_inc(q["spot_free"], 1)
                    own.settle(summed)
                    topped = own.did(v.tensor_reduce(top, s4, AX.X, ALU.max))
                    v.wait_ge(q["counted"], i + 1)
                    add_counts(0)
                    own.settle(topped)
                    v.tensor_tensor(s4, s4, over(top, [TP, T, H]), ALU.subtract).then_inc(q["soft"], 1)
                    add_counts(1)
                    v.wait_ge(q["proj"], i + 1)
                    v.tensor_tensor(S.hpT[:, bass.ds(before, W)], S.hpT[:, bass.ds(before, W)], S.ps[0:D, 3584:3584 + W],
                                    ALU.add).then_inc(q["proj_free"], 1)
                    v.wait_ge(q["expo"], i + 1)
                    own.step(v.tensor_reduce(top, e4, AX.X, ALU.add))
                    own.step(v.reciprocal(top, top))
                    own.step(v.tensor_tensor(a4, e4, over(top, [TP, T, H]), ALU.mult))
                    shape = [TP, HT, H, W]
                    for hf in range(2):
                        v.wait_ge(q["ao_free"], 2 * i + hf + 3)
                        t0 = hf * HT
                        v.tensor_tensor(AO[0:TP, hf, :, :, :], at[0:TP, t0:t0 + HT, :].unsqueeze(2).to_broadcast(shape),
                                        a4[:, t0:t0 + HT, :].unsqueeze(3).to_broadcast(shape), ALU.mult).then_inc(q["ao"], 1)
                    assert own.n == STEPS + s, (own.n, s)
            n = pairs_of(v)
            b = v.value_load(last[0:1, 0:1], min_val=0, max_val=NP - W)
            v.wait_ge(q["proj"], n * 2 + 1)
            v.tensor_tensor(S.hpT[:, bass.ds(b, W)], S.hpT[:, bass.ds(b, W)], S.ps[0:D, 3584:3584 + W], ALU.add)

        @block.scalar
        def _(act):
            act.sem_inc(q["u_free"], 1)
            act.wait_ge(q["u_zero"], 1)
            act.sem_inc(q["ucopy"], 1)
            with act.Fori(0, pairs_of(act)) as j:
                for s in range(2):
                    i = j * 2 + s
                    act.wait_ge(q["soft"], i + 1)
                    nc.scalar.activation(expo, score, ACT.Exp).then_inc(q["expo"], 1)
                    act.wait_ge(q["u"], i + 1)
                    act.wait_ge(q["proj"], i + 1)
                    act.copy(U[:, :], S.ps[0:D, 3072:3072 + H * W]).then_inc(q["ucopy"], 1)
                    act.wait_ge(q["ucopy"], i + 2)
                    act.sem_inc(q["u_free"], 1)

        @block.tensor
        def _(pe):
            pe.sem_inc(q["window_free"], 2)
            pe.sem_inc(q["lo_free"], 1)
            pe.sem_inc(q["hot_free"], 2)
            pe.sem_inc(q["ao_free"], 4)

            def project():
                for h in range(H):
                    mm = pe.matmul(S.ps[0:D, 3584:3584 + W], S.Mo[:, h * D:(h + 1) * D], U[:, h * W:(h + 1) * W],
                                   start=(h == 0), stop=(h == H - 1))
                mm.then_inc(q["proj"], 1)

            with pe.Fori(0, pairs_of(pe)) as j:
                for s in range(2):
                    i = j * 2 + s
                    pe.wait_ge(q["there"], i + 2)
                    pe.wait_ge(q[f"rwin{s}"], j * 16 + 16)
                    for t in range(T):
                        if t % HT == 0:
                            pe.wait_ge(q["scores_free"], 2 * i + t // HT + 1)
                        mm = pe.matmul(S.ps[0:TP, t * 256:(t + 1) * 256],
                                       there[:, s, :].rearrange("k (p t) -> k t p", t=T)[:, t, :], rwin[:, s, :],
                                       start=True, stop=True, skip_group_check=True)
                        if t % HT == HT - 1:
                            mm.then_inc(q["scores"], 1)
                    pe.wait_ge(q["scores"], 2 * i + 2)
                    pe.sem_inc(q["window_free"], 1)
                    pe.wait_ge(q["ucopy"], i + 1)
                    pe.wait_ge(q["proj_free"], i + 1)
                    pe.sem_inc(q["carrier"], 1)
                    project()
                    pe.wait_ge(q["lo"], i + 1)
                    pe.wait_ge(q["count_free"], 2 * i + 2)
                    for t in range(T):
                        pe.wait_ge(q["hot"], T * i + t + 1)
                        pe.matmul(S.ps[:, 2048:2048 + 500], lo[0:TP, t, :], hot[0:TP, t % 2, 0:500],
                                  start=(t == 0), stop=(t == T - 1))
                        pe.matmul(S.ps[:, 2560:2560 + 500], lo[0:TP, t, :], hot[0:TP, t % 2, 500:1000],
                                  start=(t == 0), stop=(t == T - 1)).then_inc(q["hot_free"], 1)
                    pe.wait_ge(q["hot_free"], T * i + T + 2)
                    pe.sem_inc(q["lo_free"], 1)
                    pe.sem_inc(q["counted"], 1)
                    pe.wait_ge(q["u_free"], i + 1)
                    for t in range(T):
                        if t % HT == 0:
                            pe.wait_ge(q["ao"], 2 * i + t // HT + 1)
                        mm = pe.matmul(S.ps[0:D, 3072:3072 + H * W], hsrc[0:TP, s, t, :],
                                       AO[0:TP, t // HT, t % HT, :, :].rearrange("p h w -> p (h w)"),
                                       start=(t == 0), stop=(t == T - 1))
                        if t % HT == HT - 1:
                            mm.then_inc(q["ao_free"], 1)
                    pe.wait_ge(q["ao_free"], 2 * i + 6)
                    pe.sem_inc(q["u"], 1)
            n = pairs_of(pe)
            pe.wait_ge(q["ucopy"], n * 2 + 1)
            pe.wait_ge(q["proj_free"], n * 2 + 1)
            pe.sem_inc(q["carrier"], 1)
            project()


def turn(nc, I, S, sb, sem):
    f3 = [P, NB, D]
    X, Hn, Y, tmp = (sb(n, f3, F32)[:, :, :] for n in ("t_x", "t_h", "t_y", "t_tmp"))
    st = sb("t_st", [P, 4, NB], F32)[:, :, :]
    deg = sb("t_deg", [P, 4, NB], F32)
    gam = sb("t_gam", [P, 2, D], F32)
    ones = sb("t_ones", [P, 1], BF16)
    q = {n: sem("t_" + n) for n in (
        "x", "h", "gam", "own", "pair", "pair_free_v", "pair_free_a", "hpt", "hpt_free", "one", "var", "root", "turned",
        "deg", "rdeg", "rootd", "store", "stored", "var2", "root2", "hdone", "pads", "all")}
    steps = (NB - 1) // 2
    assert NB % 2 == 1 and steps % 6 == 0

    def block_at(r, c):
        return S.A[:, bass.ds(r * NP + c * P, P)]

    with nc.Block() as block:

        @block.sync
        def _(sp):
            sp.dma_start(Hn, S.h0.rearrange("(b p) f -> p b f", p=P)).then_inc(q["h"], 16)
            sp.wait_ge(q["pads"], 1)
            sp.dma_start(X[:, 0:NB - 1, :], I["x"][0:(NB - 1) * P, :].rearrange("(b p) f -> p b f", p=P)).then_inc(q["x"], 16)
            sp.dma_start(X[0:LAST, NB - 1, :], I["x"][(NB - 1) * P:N, :]).then_inc(q["x"], 16)
            sp.dma_start(gam[:, 0, :], I["L0_gnn_gamma"].unsqueeze(0).to_broadcast([P, D])).then_inc(q["gam"], 16)
            sp.dma_start(gam[:, 1, :], I["L0_gnn_beta"].unsqueeze(0).to_broadcast([P, D])).then_inc(q["gam"], 16)
            sp.wait_ge(q["store"], 1)
            sp.dma_start(S.xs.rearrange("(b p) f -> p b f", p=P), X).then_inc(q["stored"], 16)
            sp.wait_ge(q["hdone"], 1)
            sp.dma_start(S.hs.rearrange("(b p) f -> p b f", p=P), Hn).then_inc(q["stored"], 16)
            sp.wait_ge(q["stored"], 32)

        @block.tensor
        def _(pe):
            for b in range(NB):
                if b % 8 == 0 and b >= 16:
                    pe.wait_ge(q["hpt_free"], b // 8 - 1)
                mm = pe.transpose(S.ps[:, 3072 + 512 * (b // 8 % 2) + D * (b % 8):3072 + 512 * (b // 8 % 2) + D * (b % 8) + D],
                                  S.hpT[:, b * P:(b + 1) * P], S.ident[0:D, 0:D])
                if b % 8 == 7 or b == NB - 1:
                    mm.then_inc(q["hpt"], 1)
            with pe.Fori(0, NB) as i:
                for k in range(1, steps + 1):
                    m = k - 1
                    j = (i + k) % NB
                    pe.wait_ge(q["pair_free_v" if m % 2 == 0 else "pair_free_a"], i * (steps // 2) + m // 2 + 1)
                    o = S.bank[m % 6]
                    pe.matmul(o[:, 0:P], block_at(i, j), S.identb[:, :], start=True, stop=True)
                    pe.matmul(o[:, P:2 * P], block_at(j, i), S.identb[:, :], start=True, stop=True).then_inc(q["pair"], 1)
            pe.wait_ge(q["pair_free_v"], NB * steps // 2 + 3)
            pe.wait_ge(q["pair_free_a"], NB * steps // 2 + 3)
            for n in range(7):
                for b in range(4 * n, min(4 * n + 4, NB)):
                    if b % 4 == 0 and n >= 6:
                        pe.wait_ge(q["one"], n - 5)
                    mm = pe.matmul(S.bank[n % 6][:, (b % 4) * P:(b % 4 + 1) * P], S.A[:, b * (NP + P):b * (NP + P) + P],
                                   S.identb[:, :], start=True, stop=True)
                mm.then_inc(q["all"], 1)
            pe.wait_ge(q["one"], 7)
            with pe.Fori(0, NB) as i:
                for j in range(NB):
                    mm = pe.matmul(S.bank[0][:, bass.ds(i, 1)], block_at(j, i), ones[:, :], start=(j == 0), stop=(j == NB - 1))
                mm.then_inc(q["turned"], 1)

        def unload(eng, copy, par):
            own = q["pair_free_v" if par == 0 else "pair_free_a"]
            with eng.Fori(0, NB) as i:
                for k in range(1 + par, steps + 1, 2):
                    m = k - 1
                    j = (i + k) % NB
                    eng.wait_ge(q["pair"], i * steps + m + 1)
                    copy(block_at(j, i), S.bank[m % 6][:, 0:P])
                    copy(block_at(i, j), S.bank[m % 6][:, P:2 * P]).then_inc(own, 1)

        @block.scalar
        def _(act):
            act.sem_inc(q["pair_free_a"], 3)
            unload(act, act.copy, 1)
            act.wait_ge(q["var"], 1)
            root(nc, st, NB).then_inc(q["root"], 1)
            act.wait_ge(q["var2"], 1)
            root(nc, st, NB).then_inc(q["root2"], 1)
            act.wait_ge(q["rdeg"], 1)
            nc.scalar.activation(deg[:, 2, :], deg[:, 1, :], ACT.Sqrt).then_inc(q["rootd"], 1)

        @block.vector
        def _(v):
            own = Own(v, q["own"])
            v.sem_inc(q["pair_free_v"], 3)
            v.memset(X[:, NB - 1, :], 0.0).then_inc(q["pads"], 1)
            own.did(v.memset(ones[:, :], 1.0))
            v.wait_ge(q["h"], 16)
            for n in range(4):
                v.wait_ge(q["hpt"], n + 1)
                c = min(8, NB - 8 * n)
                v.tensor_tensor(Y[:, 8 * n:8 * n + c, :], Hn[:, 8 * n:8 * n + c, :],
                                S.bank[6 + n % 2][:, 0:c * D].rearrange("p (b f) -> p b f", f=D), ALU.add).then_inc(q["hpt_free"], 1)
            v.wait_ge(q["hpt_free"], 4)
            unload(v, v.tensor_copy, 0)
            for n in range(7):
                v.wait_ge(q["all"], n + 1)
                for b in range(4 * n, min(4 * n + 4, NB)):
                    op = v.tensor_copy(S.A[:, b * (NP + P):b * (NP + P) + P], S.bank[n % 6][:, (b % 4) * P:(b % 4 + 1) * P])
                op.then_inc(q["one"], 1)
            v.wait_ge(q["one"], 7)

            def turn_of(var, done):
                def f():
                    v.sem_inc(q[var], 1)
                    v.wait_ge(q[done], 1)
                return f

            norm_steps(nc, own, Y, Hn, tmp, st, D, False, turn_of("var", "root"))
            v.wait_ge(q["gam"], 32)
            v.wait_ge(q["x"], 32)
            row = lambda k: gam[:, k, :].unsqueeze(1).to_broadcast(f3)
            own.step(v.tensor_tensor(tmp, tmp, row(0), ALU.mult))
            own.step(v.tensor_tensor(tmp, tmp, row(1), ALU.add))
            own.step(v.tensor_tensor(X, X, tmp, ALU.add))
            v.sem_inc(q["store"], 1)
            norm_steps(nc, own, X, Hn, tmp, st, D, True, turn_of("var2", "root2"))
            v.sem_inc(q["hdone"], 1)
            tb = Y.rearrange("p b f -> p (b f)").bitcast(BF16).rearrange("p (b n) -> p b n", n=P)
            wide = [P, NB - 1, P]
            own.did(v.tensor_tensor(tb[:, 0:NB - 1, :], S.A[:, 0:(NB - 1) * (NP + P)].rearrange("p (b n) -> p b n", n=NP + P)[:, :, 0:P],
                                    S.identb[:, :].unsqueeze(1).to_broadcast(wide), ALU.mult))
            own.step(v.tensor_tensor(tb[:, NB - 1, :], S.A[:, (NB - 1) * (NP + P):NB * NP], S.identb[:, :], ALU.mult))
            own.step(v.tensor_reduce(deg[:, 3, :], tb, AX.X, ALU.add))
            v.wait_ge(q["turned"], NB)
            own.step(v.tensor_tensor(deg[:, 0, :], S.bank[0][:, 0:NB], deg[:, 3, :], ALU.subtract))
            own.step(v.tensor_scalar(deg[:, 1, :], deg[:, 0, :], 1.0, None, ALU.max))
            own.step(v.reciprocal(deg[:, 1, :], deg[:, 1, :]))
            v.sem_inc(q["rdeg"], 1)
            own.step(v.tensor_scalar(deg[:, 0, :], deg[:, 0, :], 0.0, None, ALU.is_gt))
            v.wait_ge(q["rootd"], 1)
            own.step(v.tensor_tensor(S.dinv[:, 0, :], deg[:, 2, :], deg[:, 0, :], ALU.mult))
            own.did(v.tensor_scalar(S.dinv[:, 1, :], S.dinv[:, 0, :], 2.0, None, ALU.mult))
            own.step(v.tensor_tensor(S.dinv[:, 2, :], S.dinv[:, 0, :], deg[:, 3, :], ALU.mult))


def split3(nc, own, src, parts):
    v = nc.vector
    own.step(v.tensor_copy(parts[:, :, 0, :], src))
    own.step(v.tensor_tensor(src, src, parts[:, :, 0, :], ALU.subtract))
    own.step(v.tensor_copy(parts[:, :, 1, :], src))
    own.step(v.tensor_tensor(parts[:, :, 2, :], src, parts[:, :, 1, :], ALU.subtract))


def linear_pe(nc, S, q, srcs, XT, weights, width):
    pe = nc.tensor
    K = srcs[0].shape[2]
    for b in range(NB + 1):
        if b < NB:
            if b >= 2:
                pe.wait_ge(q["lin_t"], b - 1)
            for k, x in enumerate(srcs):
                mm = pe.transpose(S.bank[6 + b % 2][0:K, k * P:(k + 1) * P], x[:, b, :], S.ident[:, :])
            mm.then_inc(q["lin_tp"], 1)
        if b >= 1:
            c = b - 1
            pe.wait_ge(q["lin_t"], c + 1)
            if c >= 2:
                pe.wait_ge(q["lin_used"], c - 1)
            for k in range(len(srcs)):
                mm = pe.matmul(S.bank[4 + c % 2][:, 0:width], XT[0:K, c % 2, k * P:(k + 1) * P], weights[k],
                               start=(k == 0), stop=(k == len(srcs) - 1))
            mm.then_inc(q["lin"], 1)


def linear_act(nc, S, q, n, K, XT):
    act = nc.scalar
    for b in range(NB):
        act.wait_ge(q["lin_tp"], b + 1)
        if b >= 2:
            act.wait_ge(q["lin"], b - 1)
        act.copy(XT[0:K, b % 2, 0:n * P], S.bank[6 + b % 2][0:K, 0:n * P]).then_inc(q["lin_t"], 1)


LINEAR = ("lin_t", "lin_tp", "lin", "lin_used")


def chebyshev(nc, I, S, sb, sem):
    f3 = [P, NB, D]
    X, T0, T1, T2, tmp = (sb(n, f3, F32)[:, :, :] for n in ("c_x", "c_0", "c_1", "c_2", "c_tmp"))
    parts = sb("c_parts", [P, NB, SP3, D], BF16)[:, :, :, :]
    red = sb("c_red", [P, 2, D], F32)
    XT = sb("c_XT", [D, 2, 3 * P], F32)
    Wc = sb("c_w", [D, 2, 3, D], F32)
    bias = sb("c_b", [P, 2, D], F32)
    st = sb("c_st", [P, 4, NB], F32)[:, :, :]
    UN = 5
    assert NB % UN == 0
    q = {n: sem("c_" + n) for n in ("x", "h", "w", "own", "ready", "var", "root", "xdone", "hdone", "stored", "blk")}
    props = [{n: sem(f"c_{n}{k}") for n in ("prod", "free", "own")} for k in range(4)]
    lins = [{n: sem(f"c_{n}{k}") for n in LINEAR} for k in range(2)]

    with nc.Block() as block:

        @block.sync
        def _(sp):
            sp.dma_start(T0, S.hs.rearrange("(b p) f -> p b f", p=P)).then_inc(q["h"], 16)
            sp.dma_start(X, S.xs.rearrange("(b p) f -> p b f", p=P)).then_inc(q["x"], 16)
            for k, (w, b) in enumerate(((I["L1_gnn_W0"], I["L1_gnn_b0"]), (I["L1_gnn_W1"], I["L1_gnn_b1"]))):
                sp.dma_start(Wc[:, k, :, :], w.rearrange("k i o -> i k o")).then_inc(q["w"], 16)
                sp.dma_start(bias[:, k, :], b.unsqueeze(0).to_broadcast([P, D])).then_inc(q["w"], 16)
            sp.wait_ge(q["xdone"], 1)
            sp.dma_start(S.x2.rearrange("(b p) f -> p b f", p=P), X).then_inc(q["stored"], 16)
            sp.wait_ge(q["hdone"], 1)
            sp.dma_start(S.h2.rearrange("(b p) f -> p b f", p=P), T0).then_inc(q["stored"], 16)
            sp.dma_start(S.h3[0:NP].rearrange("(b p) s f -> p b (s f)", p=P), parts.rearrange("p b s f -> p b (s f)")).then_inc(q["stored"], 16)
            sp.dma_start(S.h3[NP:NPW].rearrange("n s f -> n (s f)"), T1[0:W, 0:2, :].rearrange("p b f -> p (b f)").bitcast(BF16)[:, 0:SP3 * D]).then_inc(q["stored"], 16)
            for a in range(NACC):
                sp.dma_start(S.acc[a][0:NP].rearrange("(b p) f -> p b f", p=P), T1).then_inc(q["stored"], 16)
                sp.dma_start(S.acc[a][NP:ACCR], T1[:, 0, :]).then_inc(q["stored"], 16)
            sp.wait_ge(q["stored"], 64 + 32 * NACC)

        @block.tensor
        def _(pe):
            for c in range(2):
                for k in range(2):
                    p = props[2 * c + k]
                    pe.wait_ge(q["ready"], 2 * c + k + 1)
                    with pe.Fori(0, NB // UN) as i:
                        for m in range(UN):
                            pe.wait_ge(p["free"], i * UN + m + 1)
                            for j in range(NB):
                                mm = pe.matmul(S.bank[m][:, 0:SP3 * D], S.A[:, bass.ds(i * (UN * P) + (j * NP + m * P), P)],
                                               parts[:, j, :, :].rearrange("p s f -> p (s f)"), start=(j == 0), stop=(j == NB - 1))
                            mm.then_inc(p["prod"], 1)
                pe.wait_ge(q["blk"], c + 1)
                pe.wait_ge(q["w"], 64)
                linear_pe(nc, S, lins[c], [T0, T1, T2], XT, [Wc[:, c, k, :] for k in range(3)], D)

        @block.scalar
        def _(act):
            for c in range(2):
                linear_act(nc, S, lins[c], 3, D, XT)
            act.wait_ge(q["var"], 1)
            root(nc, st, NB).then_inc(q["root"], 1)

        @block.vector
        def _(v):
            own = Own(v, q["own"])
            v.wait_ge(q["h"], 16)
            for c in range(2):
                for k, (src, out) in enumerate(((T0, T1), (T1, T2))):
                    p = props[2 * c + k]
                    v.sem_inc(p["free"], UN)
                    own.step(v.tensor_tensor(tmp, src, over(S.dinv[:, 0, :], f3), ALU.mult))
                    split3(nc, own, tmp, parts)
                    v.sem_inc(q["ready"], 1)
                    sf = src.rearrange("p b f -> p (b f)")
                    of = out.rearrange("p b f -> p (b f)")
                    with v.Fori(0, NB // UN) as i:
                        mine = Own(v, p["own"], i * (UN * 3))
                        for m in range(UN):
                            b = i * UN + m
                            cols = bass.ds(i * (UN * D) + m * D, D)
                            v.wait_ge(p["prod"], b + 1)
                            mine.step(v.tensor_reduce(red[:, m % 2, :], S.bank[m][:, 0:SP3 * D].rearrange("p (s f) -> p f s", s=SP3),
                                                      AX.X, ALU.add))
                            v.sem_inc(p["free"], 1)
                            mine.step(v.scalar_tensor_tensor(red[:, m % 2, :], sf[:, cols], S.dinv[:, 2, bass.ds(b, 1)],
                                                             red[:, m % 2, :], ALU.mult, ALU.subtract))
                            if k == 0:
                                mine.step(v.tensor_scalar(of[:, cols], red[:, m % 2, :], S.dinv[:, 0, bass.ds(b, 1)], None, ALU.mult))
                            else:
                                mine.step(v.scalar_tensor_tensor(of[:, cols], red[:, m % 2, :], S.dinv[:, 1, bass.ds(b, 1)],
                                                                 T0.rearrange("p b f -> p (b f)")[:, cols], ALU.mult, ALU.subtract))
                        assert mine.n == UN * 3
                v.sem_inc(q["blk"], 1)
                v.wait_ge(q["w"], 64)
                for b in range(NB):
                    v.wait_ge(lins[c]["lin"], b + 1)
                    own.step(v.tensor_tensor(T0[:, b, :], S.bank[4 + b % 2][:, 0:D], bias[:, c, :], ALU.add))
                    v.sem_inc(lins[c]["lin_used"], 1)
                    own.step(v.tensor_scalar(T0[:, b, :], T0[:, b, :], 0.0, None, ALU.max))
            v.wait_ge(q["x"], 16)
            own.did(v.memset(T1, 0.0))
            own.step(v.tensor_tensor(X, X, T0, ALU.add))
            v.sem_inc(q["xdone"], 1)

            def act_turn():
                v.sem_inc(q["var"], 1)
                v.wait_ge(q["root"], 1)

            norm_steps(nc, own, X, T0, tmp, st, D, True, act_turn)
            own.step(v.tensor_copy(tmp, T0))
            split3(nc, own, tmp, parts)
            v.sem_inc(q["hdone"], 1)


def messages(nc, I, S, sb, sem):
    spot = sb("m_spot", [P, 2, 2], I32)
    scol = sb("m_scol", [P, 2, T], I32)
    dcol = sb("m_dcol", [P, 2, T], I32)
    dstrow = sb("m_dstrow", [KW, GE], I32)
    srcrow = sb("m_srcrow", [TP, GE], I32)
    hwin = sb("m_hwin", [KW, 2, D], BF16)
    feat = sb("m_feat", [TP, 2, T, D], F32)
    there = sb("m_there", [KW, 2, GE], BF16)
    same = sb("m_same", [TP, 2, T, TP], F32)
    before = sb("m_before", [P, TP], F32)
    junk = sb("m_junk", [TP, T, TP], F32)
    xin = sb("m_xin", [TP, T, D], F32)
    msg = sb("m_msg", [TP, 2, T, D], F32)
    total = sb("m_total", [P, 2, T, D], F32)
    to = sb("m_to", [P, 2, T], I32)
    small = sb("m_small", [P, 6, T], F32)
    spare = sb("m_spare", [P, 1], F32)
    sparei = sb("m_sparei", [P, T], I32)
    thr = sb("m_thr", [P, 1], F32)
    dl, inside, cnt, gap, ge0 = (small[0:TP, k, :] for k in range(5))
    valid = sb("m_valid", [TP, 2, T], F32)

    q = {n: sem("m_" + n) for n in (
        "spot0", "spot1", "scol0", "scol1", "dcol0", "dcol1", "hwin0", "hwin1", "feat0", "feat1", "dstrow", "srcrow",
        "cols_free", "dstrow_free", "srcrow_free", "window_free", "feat_free", "there", "near", "near_free", "x", "x_free",
        "msg", "msg_free", "same", "same_free", "sum", "sum_free", "total", "total_free", "to", "own", "carrier", "const",
        "const2", "valid_free")}
    added = [sem(f"m_added{a}") for a in range(NACC)]
    STEPS = 13

    def pairs_of(eng):
        return eng.value_load(S.count[0:1, 1:2], min_val=1, max_val=P * IC // 2)

    with nc.Block() as block:

        @block.sync
        def _(sp):
            with sp.Fori(0, pairs_of(sp)) as j:
                for s in range(2):
                    i = j * 2 + s
                    g = sp.value_load(S.items[bass.ds(i, 1), 0:1], min_val=0, max_val=G - 1)
                    b = sp.value_load(S.items[bass.ds(i, 1), 1:2], min_val=0, max_val=NP - W)
                    sp.wait_ge(q["cols_free"], i + 1)
                    sp.dma_start(spot[:, s, :], S.items[bass.ds(i, 1), :].to_broadcast([P, 2])).then_inc(q[f"spot{s}"], 16)
                    sp.dma_start(dcol[0:TP, s, :], I["dst"][bass.ds(g * GE, GE)].rearrange("(p t) -> p t", t=T)).then_inc(q[f"dcol{s}"], 16)
                    sp.dma_start(scol[0:TP, s, :], I["src"][bass.ds(g * GE, GE)].rearrange("(p t) -> p t", t=T)).then_inc(q[f"scol{s}"], 16)
                    sp.wait_ge(q["window_free"], i + 1)
                    sp.dma_start(hwin[:, s, :], S.h3[bass.ds(b, W)].rearrange("n s f -> (n s) f")).then_inc(q[f"hwin{s}"], 16)
                    sp.wait_ge(q["feat_free"], i + 1)
                    sp.dma_start(feat[:, s, :, :], I["edge_attr_64"][bass.ds(g * GE, GE), :].rearrange("(p t) f -> p t f", t=T)).then_inc(q[f"feat{s}"], 16)
                    sp.wait_ge(q["dstrow_free"], i + 1)
                    sp.dma_start(dstrow[:, :], I["dst"][bass.ds(g * GE, GE)].unsqueeze(0).to_broadcast([KW, GE])).then_inc(q["dstrow"], 16)
                    sp.wait_ge(q["srcrow_free"], i + 1)
                    sp.dma_start(srcrow[:, :], I["src"][bass.ds(g * GE, GE)].unsqueeze(0).to_broadcast([TP, GE])).then_inc(q["srcrow"], 16)

        @block.gpsimd
        def _(g):
            g.iota(sparei[:, :], pattern=[[0, T]], base=NP, channel_multiplier=1).then_inc(q["const"], 1)
            g.memset(total[:, :, :, :], 0.0).then_inc(q["const"], 1)
            g.memset(before[:, :], 1.0).then_inc(q["const"], 1)
            g.wait_ge(q["const"], 3)
            g.affine_select(out=before[:, :], in_=before[:, :], compare_op=ALU.is_gt, fill=0.0, base=0,
                            pattern=[[-1, TP]], channel_multiplier=1).then_inc(q["const2"], 1)
            for a in range(NACC):
                g.indirect_dma_start(out=S.acc[a], out_offset=bass.IndirectOffsetOnAxis(ap=sparei[:, 0:1], axis=0),
                                     in_=total[:, 0, 0, :], in_offset=None, compute_op=ALU.add).then_inc(added[a], 16)
            for a in range(NACC):
                g.wait_ge(added[a], 16)
            g.sem_inc(q["total_free"], 1)
            n = pairs_of(g)
            with g.Fori(0, n) as j:
                for s in range(2):
                    i = j * 2 + s
                    g.wait_ge(q["total"], i + 1)
                    g.wait_ge(q["to"], i + 1)
                    for t in range(T):
                        if t == NACC:
                            g.sem_inc(q["total_free"], 1)
                        g.wait_ge(added[t % NACC], i * (16 * T // NACC) + 16 + 16 * (t // NACC))
                        g.sem_inc(q["carrier"], 1)
                        g.indirect_dma_start(out=S.acc[t % NACC], out_offset=bass.IndirectOffsetOnAxis(ap=to[:, s, t:t + 1], axis=0),
                                             in_=total[:, s, t, :], in_offset=None, compute_op=ALU.add).then_inc(added[t % NACC], 16)
            for a in range(NACC):
                g.wait_ge(added[a], n * (2 * 16 * T // NACC) + 16)
            g.sem_inc(q["carrier"], 1)

        @block.vector
        def _(v):
            for n, k in (("cols_free", 2), ("feat_free", 2), ("dstrow_free", 1), ("srcrow_free", 1), ("near_free", 2)):
                v.sem_inc(q[n], k)
            v.wait_ge(q["const"], 3)
            first = Own(v, q["own"])
            first.did(v.tensor_copy(spare[:, :], sparei[:, 0:1]))
            first.did(v.tensor_copy(to[:, :, :], sparei[:, :].unsqueeze(1).to_broadcast([P, 2, T])))
            v.wait_ge(q["const2"], 1)
            with v.Fori(0, pairs_of(v)) as j:
                for s in range(2):
                    i = j * 2 + s
                    own = Own(v, q["own"], i * STEPS + 2)
                    v.wait_ge(q[f"spot{s}"], j * 16 + 16)
                    own.did(v.tensor_scalar(thr[0:KW, :], S.thirdf[0:KW, :], spot[0:KW, s, 1:2], None, ALU.add))
                    v.wait_ge(q[f"dcol{s}"], j * 16 + 16)
                    own.step(v.tensor_scalar(dl, dcol[0:TP, s, :], spot[0:TP, s, 1:2], None, ALU.subtract))
                    own.step(v.tensor_scalar(ge0, dl, 0.0, None, ALU.is_ge))
                    v.wait_ge(q["msg_free"], i + 1)
                    own.did(v.scalar_tensor_tensor(valid[:, s, :], dl, float(W), ge0, ALU.is_lt, ALU.mult))
                    v.wait_ge(q["window_free"], i + 1)
                    v.wait_ge(q["dstrow"], i * 16 + 16)
                    own.step(v.tensor_scalar(there[:, s, :], dstrow[:, :], thr[0:KW, :], None, ALU.is_equal))
                    v.sem_inc(q["dstrow_free"], 1)
                    v.sem_inc(q["there"], 1)
                    v.wait_ge(q[f"scol{s}"], j * 16 + 16)
                    v.wait_ge(q["srcrow"], i * 16 + 16)
                    v.wait_ge(q["same_free"], i + 1)
                    full = [TP, T, TP]
                    own.step(v.tensor_tensor(same[:, s, :, :], srcrow[:, :].rearrange("k (p t) -> k t p", t=T),
                                             over(scol[0:TP, s, :], full), ALU.is_equal))
                    v.sem_inc(q["srcrow_free"], 1)
                    v.sem_inc(q["same"], 1)
                    own.step(v.tensor_tensor(junk[:, :, :], same[:, s, :, :], before[0:TP, :].unsqueeze(1).to_broadcast(full), ALU.mult))
                    own.step(v.tensor_reduce(cnt, junk[:, :, :], AX.X, ALU.add))
                    v.wait_ge(q["near"], i + 1)
                    v.wait_ge(q[f"feat{s}"], j * 16 + 16)
                    v.wait_ge(q["x_free"], i + 1)
                    own.did(v.tensor_tensor(xin[:, :, :], S.bank[s][0:TP, :].rearrange("p (t f) -> p t f", t=T),
                                            feat[:, s, :, :], ALU.add))
                    own.step(v.tensor_scalar(cnt, cnt, 1.0, None, ALU.min))
                    v.sem_inc(q["feat_free"], 1)
                    v.sem_inc(q["near_free"], 1)
                    v.sem_inc(q["x"], 1)
                    own.step(v.tensor_scalar(gap, scol[0:TP, s, :], -1.0, spare[0:TP, :], ALU.mult, ALU.add))
                    own.step(v.tensor_tensor(gap, gap, cnt, ALU.mult))
                    v.wait_ge(q["total_free"], i + 1)
                    own.step(v.tensor_tensor(to[0:TP, s, :], gap, scol[0:TP, s, :], ALU.add))
                    v.sem_inc(q["to"], 1)
                    v.sem_inc(q["cols_free"], 1)
                    assert own.n == STEPS, own.n

        @block.scalar
        def _(act):
            act.sem_inc(q["x_free"], 1)
            act.sem_inc(q["msg_free"], 2)
            with act.Fori(0, pairs_of(act)) as j:
                for s in range(2):
                    i = j * 2 + s
                    act.wait_ge(q["x"], i + 1)
                    act.wait_ge(q["sum_free"], i + 1)
                    for t in range(T):
                        op = nc.scalar.activation(msg[:, s, t, :], xin[:, t, :], ACT.Relu, scale=valid[:, s, t:t + 1])
                    op.then_inc(q["msg"], 1)
                    act.wait_ge(q["msg"], i + 1)
                    act.sem_inc(q["x_free"], 1)
                    act.sem_inc(q["msg_free"], 1)
                    act.wait_ge(q["sum"], i + 1)
                    act.wait_ge(q["total_free"], i + 1)
                    act.copy(total[0:TP, s, :, :], S.bank[2 + s][0:TP, :].rearrange("p (t f) -> p t f", t=T)).then_inc(q["total"], 1)

        @block.tensor
        def _(pe):
            pe.sem_inc(q["window_free"], 2)
            pe.sem_inc(q["same_free"], 2)
            pe.sem_inc(q["sum_free"], 2)
            with pe.Fori(0, pairs_of(pe)) as j:
                for s in range(2):
                    i = j * 2 + s
                    pe.wait_ge(q["there"], i + 1)
                    pe.wait_ge(q[f"hwin{s}"], j * 16 + 16)
                    pe.wait_ge(q["near_free"], i + 1)
                    for t in range(T):
                        mm = pe.matmul(S.bank[s][0:TP, t * D:(t + 1) * D],
                                       there[:, s, :].rearrange("k (p t) -> k t p", t=T)[:, t, :], hwin[:, s, :],
                                       start=True, stop=True, skip_group_check=True)
                    mm.then_inc(q["near"], 1)
                    pe.wait_ge(q["near"], i + 1)
                    pe.sem_inc(q["window_free"], 1)
                    pe.wait_ge(q["same"], i + 1)
                    pe.wait_ge(q["msg"], i + 1)
                    for t in range(T):
                        mm = pe.matmul(S.bank[2 + s][0:TP, t * D:(t + 1) * D], same[:, s, t, :], msg[:, s, t, :],
                                       start=True, stop=True, skip_group_check=True)
                    mm.then_inc(q["sum"], 1)
                    pe.wait_ge(q["sum"], i + 1)
                    pe.sem_inc(q["same_free"], 1)
                    pe.sem_inc(q["sum_free"], 1)


def mlp(nc, I, S, sb, sem):
    f3 = [P, NB, D]
    X, Hm = (sb(n, f3, F32)[:, :, :] for n in ("l_x", "l_h"))
    Y, tmp = (sb(n, [P, NB, 2 * D], F32)[:, :, :] for n in ("l_y", "l_tmp"))
    st = sb("l_st", [P, 4, NB], F32)[:, :, :]
    XT = sb("l_XT", [P, 2, P], F32)
    W1 = sb("l_w1", [D, 2 * D], F32)
    W2 = sb("l_w2", [2 * D, D], F32)
    rows = sb("l_rows", [P, 3, 2 * D], F32)
    b2 = sb("l_b2", [P, D], F32)
    eps = sb("l_eps", [P, 1], F32)
    fc = sb("l_fc", [D, D], F32)
    att = sb("l_att", [D, 2], F32)
    Wz = sb("l_wz", [D, D + 2], F32)
    esT = sb("l_esT", [NB, P], F32)
    accs = [Y[:, :, 0:D], Y[:, :, D:2 * D], tmp[:, :, 0:D], tmp[:, :, D:2 * D]]
    q = {n: sem("l_" + n) for n in ("x", "h", "acc", "w", "w3", "own", "var", "root", "in1", "in2", "in3", "store", "stored",
                                    "fct", "wz", "var2", "root2", "es", "est", "estc")}
    lins = [{n: sem(f"l_{n}{k}") for n in LINEAR} for k in range(3)]

    with nc.Block() as block:

        @block.sync
        def _(sp):
            by = "(b p) f -> p b f"
            sp.dma_start(Hm, S.h2.rearrange(by, p=P)).then_inc(q["h"], 16)
            sp.dma_start(eps[:, :], I["L2_gnn_eps"].unsqueeze(0).to_broadcast([P, 1])).then_inc(q["h"], 16)
            for a in range(NACC):
                sp.dma_start(accs[a], S.acc[a][0:NP].rearrange(by, p=P)).then_inc(q["acc"], 16)
            sp.dma_start(X, S.x2.rearrange(by, p=P)).then_inc(q["x"], 16)
            sp.dma_start(W1[:, :], I["L2_gnn_W1"]).then_inc(q["w"], 16)
            sp.dma_start(W2[:, :], I["L2_gnn_W2"]).then_inc(q["w"], 16)
            for k, r in enumerate((I["L2_gnn_b1"], I["L2_gnn_ln_g"], I["L2_gnn_ln_b"])):
                sp.dma_start(rows[:, k, :], r.unsqueeze(0).to_broadcast([P, 2 * D])).then_inc(q["w"], 16)
            sp.dma_start(b2[:, :], I["L2_gnn_b2"].unsqueeze(0).to_broadcast([P, D])).then_inc(q["w"], 16)
            sp.dma_start(fc[:, :], I["L3_gnn_fc_w"]).then_inc(q["w3"], 16)
            with nc.allow_non_contiguous_dma(reason="128 values, once"):
                sp.dma_start(att[:, :], I["L3_gnn_attn_w"].rearrange("o (k c) -> c (o k)", k=2)).then_inc(q["w3"], 16)
            sp.wait_ge(q["store"], 1)
            sp.dma_start(S.x3.rearrange(by, p=P), X).then_inc(q["stored"], 16)
            sp.wait_ge(q["estc"], 1)
            sp.dma_start(S.z.rearrange(by, p=P), Y[:, :, 0:D + 2]).then_inc(q["stored"], 16)
            sp.dma_start(S.es.rearrange("(b p) -> b p", p=P), esT[:, :]).then_inc(q["stored"], 16)
            sp.wait_ge(q["stored"], 48)

        @block.tensor
        def _(pe):
            pe.wait_ge(q["w3"], 32)
            pe.transpose(S.bank[0][0:D, 0:D], fc[:, :], S.ident[0:D, 0:D])
            pe.matmul(S.bank[1][0:D, 0:2], fc[:, :], att[:, :], start=True, stop=True).then_inc(q["fct"], 1)
            pe.wait_ge(q["in1"], 1)
            pe.wait_ge(q["w"], 96)
            linear_pe(nc, S, lins[0], [Hm], XT, [W1[:, :]], 2 * D)
            pe.wait_ge(q["in2"], 1)
            linear_pe(nc, S, lins[1], [Y], XT, [W2[:, :]], D)
            pe.wait_ge(q["in3"], 1)
            pe.wait_ge(q["wz"], 2)
            linear_pe(nc, S, lins[2], [Hm], XT, [Wz[:, :]], D + 2)
            pe.wait_ge(q["es"], 1)
            pe.transpose(S.bank[0][0:NB, 0:P], Y[:, :, D], S.ident[:, :]).then_inc(q["est"], 1)

        @block.scalar
        def _(act):
            act.wait_ge(q["fct"], 1)
            act.copy(Wz[:, 0:D], S.bank[0][0:D, 0:D]).then_inc(q["wz"], 1)
            act.copy(Wz[:, D:D + 2], S.bank[1][0:D, 0:2]).then_inc(q["wz"], 1)
            linear_act(nc, S, lins[0], 1, D, XT)
            act.wait_ge(q["var"], 1)
            root(nc, st, NB).then_inc(q["root"], 1)
            linear_act(nc, S, lins[1], 1, 2 * D, XT)
            act.wait_ge(q["var2"], 1)
            root(nc, st, NB).then_inc(q["root2"], 1)
            linear_act(nc, S, lins[2], 1, D, XT)
            act.wait_ge(q["est"], 1)
            act.copy(esT[:, :], S.bank[0][0:NB, 0:P]).then_inc(q["estc"], 1)

        @block.vector
        def _(v):
            own = Own(v, q["own"])
            v.wait_ge(q["h"], 32)
            v.wait_ge(q["acc"], 16 * NACC)
            own.did(v.tensor_tensor(accs[0], accs[0], accs[1], ALU.add))
            own.step(v.tensor_tensor(accs[2], accs[2], accs[3], ALU.add))
            own.step(v.tensor_tensor(accs[0], accs[0], accs[2], ALU.add))
            own.step(v.scalar_tensor_tensor(accs[0], Hm, eps[:, :], accs[0], ALU.mult, ALU.add))
            own.step(v.tensor_tensor(Hm, Hm, accs[0], ALU.add))
            v.sem_inc(q["in1"], 1)
            v.wait_ge(q["w"], 96)
            for b in range(NB):
                v.wait_ge(lins[0]["lin"], b + 1)
                v.tensor_tensor(Y[:, b, :], S.bank[4 + b % 2][:, 0:2 * D], rows[:, 0, :], ALU.add).then_inc(lins[0]["lin_used"], 1)
            v.wait_ge(lins[0]["lin_used"], NB)

            def turn_of(var, done):
                def f():
                    v.sem_inc(q[var], 1)
                    v.wait_ge(q[done], 1)
                return f

            norm_steps(nc, own, Y, Y, tmp, st, 2 * D, False, turn_of("var", "root"))
            row = lambda k: rows[:, k, :].unsqueeze(1).to_broadcast([P, NB, 2 * D])
            own.step(v.tensor_tensor(tmp, tmp, row(1), ALU.mult))
            own.step(v.tensor_tensor(tmp, tmp, row(2), ALU.add))
            own.step(v.tensor_scalar(Y, tmp, 0.0, None, ALU.max))
            v.sem_inc(q["in2"], 1)
            v.wait_ge(q["x"], 16)
            own.step(v.tensor_tensor(X, X, b2[:, :].unsqueeze(1).to_broadcast(f3), ALU.add))
            for b in range(NB):
                v.wait_ge(lins[1]["lin"], b + 1)
                v.tensor_tensor(X[:, b, :], X[:, b, :], S.bank[4 + b % 2][:, 0:D], ALU.add).then_inc(lins[1]["lin_used"], 1)
            v.wait_ge(lins[1]["lin_used"], NB)
            v.sem_inc(q["store"], 1)
            norm_steps(nc, own, X, Hm, tmp[:, :, 0:D], st, D, True, turn_of("var2", "root2"))
            v.sem_inc(q["in3"], 1)
            for b in range(NB):
                v.wait_ge(lins[2]["lin"], b + 1)
                v.tensor_copy(Y[:, b, 0:D + 2], S.bank[4 + b % 2][:, 0:D + 2]).then_inc(lins[2]["lin_used"], 1)
            v.wait_ge(lins[2]["lin_used"], NB)
            v.sem_inc(q["es"], 1)


def gat(nc, I, S, sb, sem, out):
    CUT = [0, 7, 13, 19, NB]
    NC = len(CUT) - 1
    WIDE = 7 * P
    qrow = sb("g_q", [P, NP], F32)
    mask = sb("g_mask", [P, WIDE], F32)
    prob = sb("g_prob", [P, NC, WIDE], F32)
    Z = sb("g_z", [P, NB, D + 2], F32)
    low = sb("g_low", [P, 2, WIDE], F32)
    PT = sb("g_pt", [P, 2, 4 * P], F32)
    xb = sb("g_x", [P, D], F32)
    ob = sb("g_o", [P, D], F32)
    c = sb("g_c", [P, 16], F32)
    edc = sb("g_ed", [P, NB], F32)
    q = {n: sem("g_" + n) for n in (
        "z", "es", "own", "own2", "clip", "clip_free", "prob", "weigh", "top", "top_free", "high", "pt", "ptc", "pt_used",
        "num", "num_free", "x", "x_free", "ob", "ob_free", "out", "ready", "mid")}

    def size(k):
        return (CUT[k + 1] - CUT[k]) * P

    GR = -(-NB // 4)
    with nc.Block() as block:

        @block.sync
        def _(sp):
            sp.dma_start(qrow[:, :], S.es.unsqueeze(0).to_broadcast([P, NP])).then_inc(q["es"], 16)
            sp.dma_start(Z[:, :, :], S.z.rearrange("(b p) f -> p b f", p=P)).then_inc(q["z"], 16)
            with sp.Fori(0, NB - 1) as j:
                sp.wait_ge(q["x_free"], j + 1)
                sp.dma_start(xb[:, :], S.x3[bass.ds(j * P, P), :]).then_inc(q["x"], 16)
                sp.wait_ge(q["ob"], j + 1)
                sp.dma_start(out[bass.ds(j * P, P), :], ob[:, :]).then_inc(q["out"], 16)
                sp.wait_ge(q["out"], j * 16 + 16)
                sp.sem_inc(q["ob_free"], 1)
            sp.wait_ge(q["x_free"], NB)
            sp.dma_start(xb[:, :], S.x3[(NB - 1) * P:NP, :]).then_inc(q["x"], 16)
            sp.wait_ge(q["ob"], NB)
            sp.dma_start(out[(NB - 1) * P:N, :], ob[0:LAST, :]).then_inc(q["out"], 16)
            sp.wait_ge(q["out"], NB * 16)

        @block.vector
        def _(v):
            own = Own(v, q["own"])
            v.sem_inc(q["x_free"], 1)
            v.sem_inc(q["ob_free"], 1)
            v.sem_inc(q["num_free"], 1)
            v.sem_inc(q["high"], 2)
            v.wait_ge(q["es"], 16)
            own.step(v.tensor_reduce(c[:, 0:1], qrow[:, :], AX.X, ALU.min))
            own.step(v.tensor_scalar(c[:, 1:2], c[:, 0:1], -1.0, 1.0, ALU.mult, ALU.add))
            own.step(v.tensor_scalar(qrow[:, :], qrow[:, :], c[:, 1:2], None, ALU.add))
            v.wait_ge(q["z"], 16)
            own.step(v.tensor_scalar(edc[:, :], Z[:, :, D + 1], c[:, 1:2], None, ALU.subtract))
            own.step(v.memset(Z[:, :, D], 1.0))
            v.sem_inc(q["ready"], 1)
            BOUND, END = 2 * NC + 6, 4

            def bound(mine, j):
                for k in range(NC):
                    a, n = CUT[k] * P, size(k)
                    mine.step(v.scalar_tensor_tensor(mask[:, 0:n], S.A[:, bass.ds(j * NP + a, n)], 1.0, qrow[:, a:a + n],
                                                     ALU.min, ALU.mult))
                    mine.step(v.tensor_reduce(c[:, 4 + k:5 + k], mask[:, 0:n], AX.X, ALU.max))
                v.wait_ge(q["top_free"], j + 1)
                mine.did(v.tensor_copy(c[:, 11:12], edc[:, bass.ds(j, 1)]))
                mine.step(v.tensor_reduce(c[:, 8:9], c[:, 4:4 + NC], AX.X, ALU.max))
                mine.step(v.tensor_tensor(c[:, 12:13], c[:, 8:9], c[:, 11:12], ALU.add))
                mine.step(v.scalar_tensor_tensor(c[:, 12:13], c[:, 12:13], 0.01, c[:, 12:13], ALU.mult, ALU.max))
                mine.did(v.tensor_tensor(c[:, 9:10], c[:, 11:12], c[:, 12:13], ALU.subtract))
                mine.step(v.scalar_tensor_tensor(c[:, 10:11], c[:, 11:12], 0.01, c[:, 12:13], ALU.mult, ALU.subtract))
                v.sem_inc(q["top"], 1)
                for k in range(NC):
                    a, n = CUT[k] * P, size(k)
                    v.wait_ge(q["clip_free"], j * NC + k + 1)
                    v.tensor_scalar(prob[:, k, 0:n], qrow[:, a:a + n], c[:, 8:9], None, ALU.min).then_inc(q["clip"], 1)
                for k in range(NC):
                    n = size(k)
                    v.wait_ge(q["prob"], j * NC + k + 1)
                    v.tensor_tensor(prob[:, k, 0:n], prob[:, k, 0:n], low[:, k % 2, 0:n], ALU.max).then_inc(q["high"], 1)

            def finish(mine, j):
                v.wait_ge(q["num"], j + 1)
                num = S.bank[6]
                mine.step(v.tensor_scalar(c[:, 12:13], num[:, D:D + 1], 0.0, None, ALU.is_equal))
                mine.step(v.tensor_tensor(c[:, 13:14], num[:, D:D + 1], c[:, 12:13], ALU.add))
                mine.step(v.reciprocal(c[:, 14:15], c[:, 13:14]))
                v.wait_ge(q["x"], j * 16 + 16)
                v.wait_ge(q["ob_free"], j + 1)
                mine.step(v.scalar_tensor_tensor(ob[:, :], num[:, 0:D], c[:, 14:15], xb[:, :], ALU.mult, ALU.add))
                v.sem_inc(q["num_free"], 1)
                v.sem_inc(q["ob"], 1)
                v.sem_inc(q["x_free"], 1)

            bound(Own(v, q["own2"]), 0)
            with v.Fori(0, NB - 1) as j:
                mine = Own(v, q["own2"], j * (BOUND + END) + BOUND)
                bound(mine, j + 1)
                finish(mine, j)
                assert mine.n == BOUND + END
            finish(Own(v, q["own2"], NB * BOUND + (NB - 1) * END), NB - 1)

        @block.scalar
        def _(act):
            act.sem_inc(q["top_free"], 1)
            act.wait_ge(q["ready"], 1)
            with act.Fori(0, NB) as j:
                act.wait_ge(q["top"], j + 1)
                for k in range(NC):
                    n = size(k)
                    act.wait_ge(q["clip"], j * NC + k + 1)
                    act.wait_ge(q["high"], j * NC + k + 1)
                    nc.scalar.activation(low[:, k % 2, 0:n], prob[:, k, 0:n], ACT.Exp, bias=c[:, 10:11], scale=0.01).then_inc(q["mid"], 1)
                    act.wait_ge(q["mid"], j * NC + k + 1)
                    nc.scalar.activation(prob[:, k, 0:n], prob[:, k, 0:n], ACT.Exp, bias=c[:, 9:10]).then_inc(q["prob"], 1)
                act.wait_ge(q["prob"], j * NC + NC)
                act.sem_inc(q["top_free"], 1)
                for n in range(GR):
                    act.wait_ge(q["pt"], j * GR + n + 1)
                    act.wait_ge(q["pt_used"], j * GR + n + 1)
                    w = min(4, NB - 4 * n) * P
                    act.copy(PT[:, n % 2, 0:w], S.bank[n % 4][:, 0:w]).then_inc(q["ptc"], 1)

        @block.gpsimd
        def _(g):
            with g.Fori(0, NB) as j:
                for k in range(NC):
                    a, n = CUT[k] * P, size(k)
                    g.wait_ge(q["high"], j * NC + k + 3)
                    g.tensor_tensor(prob[:, k, 0:n], prob[:, k, 0:n], S.A[:, bass.ds(j * NP + a, n)], ALU.mult).then_inc(q["weigh"], 1)

        @block.tensor
        def _(pe):
            pe.sem_inc(q["clip_free"], NC)
            pe.sem_inc(q["pt_used"], 2)
            pe.wait_ge(q["ready"], 1)
            with pe.Fori(0, NB) as j:
                def products(n):
                    pe.wait_ge(q["ptc"], j * GR + n + 1)
                    if n == 0:
                        pe.wait_ge(q["num_free"], j + 1)
                    for b in range(4 * n, min(4 * n + 4, NB)):
                        mm = pe.matmul(S.bank[6][:, 0:D + 1], PT[:, n % 2, (b % 4) * P:(b % 4 + 1) * P], Z[:, b, 0:D + 1],
                                       start=(b == 0), stop=(b == NB - 1))
                    mm.then_inc(q["pt_used"], 1)

                for n in range(GR):
                    for b in range(4 * n, min(4 * n + 4, NB)):
                        k = max(x for x in range(NC) if CUT[x] <= b)
                        if b == CUT[k]:
                            pe.wait_ge(q["weigh"], j * NC + k + 1)
                        at = (b - CUT[k]) * P
                        mm = pe.transpose(S.bank[n % 4][:, (b % 4) * P:(b % 4 + 1) * P], prob[:, k, at:at + P], S.ident[:, :])
                    mm.then_inc(q["pt"], 1)
                    if n >= 1:
                        products(n - 1)
                    done = sum(CUT[k + 1] <= 4 * n + 4 for k in range(NC)) - sum(CUT[k + 1] <= 4 * n for k in range(NC))
                    if n == GR - 1:
                        done = 1
                    if done:
                        pe.wait_ge(q["pt"], j * GR + n + 1)
                        pe.sem_inc(q["clip_free"], done)
                products(GR - 1)
                pe.wait_ge(q["pt_used"], j * GR + GR + 2)
                pe.sem_inc(q["num"], 1)


def build(nc, I, out):
    with ExitStack() as ctx:
        def sb_in(stack):
            return lambda name, shape, dt: stack.enter_context(nc.sbuf_tensor(name, shape, dt))

        taken = []

        def sem(name):
            taken.append(nc.alloc_semaphore(name))
            return taken[-1]

        def dram(name, shape, dt=F32):
            return nc.dram_tensor(name, shape, dt, kind="Internal").ap()

        keep = sb_in(ctx)
        S = Shared()
        S.A = keep("A", [P, NB * NP], BF16)
        S.ident = keep("ident", [P, P], F32)
        S.identb = keep("identb", [P, P], BF16)
        S.count = keep("count", [1, 3], I32)
        S.third = keep("third", [P, 1], I32)
        S.thirdf = keep("thirdf", [P, 1], F32)
        S.dinv = keep("dinv", [P, 3, NB], F32)
        S.ps = ctx.enter_context(nc.psum_tensor("ps", [P, 4096], F32))
        S.bank = [S.ps[:, 512 * k:512 * (k + 1)] for k in range(8)]
        S.items = dram("items", [P * IC, 2], I32)
        S.h0, S.xs, S.hs, S.x2, S.h2 = (dram(n, [NP, D]) for n in ("h0", "x1", "h1", "x2", "h2"))
        S.edges = dram("edge_table", [G, TP, 3, T])
        S.r3 = dram("r3", [NPW, SP3, H * D], BF16)
        S.h3 = dram("h3", [NPW, SP3, D], BF16)
        S.acc = [dram(f"acc{a}", [ACCR, D]) for a in range(NACC)]
        S.x3 = dram("x3", [NP, D])
        S.z = dram("z", [NP, D + 2])
        S.es = dram("es", [NP])

        with ExitStack() as layer0:
            more = sb_in(layer0)
            S.Mo = more("Mo", [D, H * D], F32)
            S.hpT = more("hpT", [D, NP], F32)
            S.ramp = more("ramp", [P, KEYS], I16)
            prepare(nc, I, S, None, sem)
            with ExitStack() as scratch:
                attend(nc, I, S, sb_in(scratch), sem)
            with ExitStack() as scratch:
                turn(nc, I, S, sb_in(scratch), sem)
        with ExitStack() as scratch:
            chebyshev(nc, I, S, sb_in(scratch), sem)
        nc.clear_and_free_semaphores(taken)
        nc.all_engine_barrier()
        for stage in (messages, mlp):
            with ExitStack() as scratch:
                stage(nc, I, S, sb_in(scratch), sem)
        with ExitStack() as scratch:
            gat(nc, I, S, sb_in(scratch), sem, out)


_INS = ['x', 'src', 'dst', 'edge_attr_64', 'L0_gnn_Wq', 'L0_gnn_Wk', 'L0_gnn_Wv', 'L0_gnn_Wo', 'L0_gnn_gamma',
        'L0_gnn_beta', 'L1_gnn_W0', 'L1_gnn_b0', 'L1_gnn_W1', 'L1_gnn_b1', 'L2_gnn_W1', 'L2_gnn_b1', 'L2_gnn_ln_g',
        'L2_gnn_ln_b', 'L2_gnn_W2', 'L2_gnn_b2', 'L2_gnn_eps', 'L3_gnn_fc_w', 'L3_gnn_attn_w']


def kernel(**inputs):
    import numpy as _np
    import concourse.bacc as _bacc
    from concourse import mybir as _mybir
    from concourse.bass_utils import run_bass_kernel_spmd as _run

    nc = _bacc.Bacc("TRN2", target_bir_lowering=False, num_devices=1)
    arrays, args = {}, {}
    for name in _INS:
        a = _np.ascontiguousarray(inputs[name])
        arrays[f"in_{name}_dram"] = a
        args[name] = nc.dram_tensor(f"in_{name}_dram", a.shape, _mybir.dt.from_np(a.dtype), kind="ExternalInput").ap()
    out = nc.dram_tensor("out_0_dram", (3125, 64), _mybir.dt.float32, kind="ExternalOutput").ap()
    build(nc, args, out)
    r = _run(nc, [arrays], core_ids=[0])
    return r.results[0]["out_0_dram"]
```

```python
from contextlib import ExitStack

import numpy as np

import concourse.bass as bass
import concourse.mybir as mybir

F32 = mybir.dt.float32
BF16 = mybir.dt.bfloat16
I32 = mybir.dt.int32
I16 = mybir.dt.int16
ALU = mybir.AluOpType
ACT = mybir.ActivationFunctionType
AX = mybir.AxisListType

P = 128
N = 3125
D = 64
E = 100000
H = 4
NB = -(-N // P)
NP = NB * P
LAST = N - (NB - 1) * P
TP = 125
T = 8
GE = TP * T
G = E // GE
W = 40
NPW = NP + W
SP3 = 3
KW = SP3 * W
KEYS = NB * W
MAXWIN = -(-N // W)
IC = 62
assert P * IC > G * MAXWIN and G * GE == E and KEYS <= 1024
EPS = 1e-5
NACC = 4
ACCR = NP + P


class Shared:
    pass


class Own:

    def __init__(self, eng, sem, base=0):
        self.eng, self.sem, self.base, self.n = eng, sem, base, 0

    def did(self, ins):
        ins.then_inc(self.sem, 1)
        self.n += 1
        return self.n

    def settle(self, step=None):
        self.eng.wait_ge(self.sem, self.base + (step or self.n))

    def step(self, ins):
        self.did(ins)
        self.settle()


def over(ap, shape):
    return ap.unsqueeze(2).to_broadcast(shape)


def norm_steps(nc, own, src, out, tmp, st, width, relu, act_turn):
    b = src.shape[1]
    full = [P, b, width]
    own.step(nc.vector.tensor_reduce(st[:, 0, 0:b], src, AX.X, ALU.add))
    own.step(nc.vector.tensor_scalar(st[:, 1, 0:b], st[:, 0, 0:b], 1.0 / width, None, ALU.mult))
    own.step(nc.vector.tensor_tensor(out, src, over(st[:, 1, 0:b], full), ALU.subtract))
    own.step(nc.vector.tensor_tensor(tmp, out, out, ALU.mult))
    own.step(nc.vector.tensor_reduce(st[:, 0, 0:b], tmp, AX.X, ALU.add))
    own.step(nc.vector.tensor_scalar(st[:, 1, 0:b], st[:, 0, 0:b], 1.0 / width, EPS, ALU.mult, ALU.add))
    own.step(nc.vector.reciprocal(st[:, 2, 0:b], st[:, 1, 0:b]))
    act_turn()
    own.step(nc.vector.tensor_tensor(tmp, out, over(st[:, 3, 0:b], full), ALU.mult))
    if relu:
        own.step(nc.vector.tensor_scalar(out, tmp, 0.0, None, ALU.max))


def root(nc, st, b):
    return nc.scalar.activation(st[:, 3, 0:b], st[:, 2, 0:b], ACT.Sqrt)


def prepare(nc, I, S, sem):
    B = S.A
    at = [0]

    def carve(cols, dt=F32):
        v = B[:, at[0]:at[0] + 2 * cols] if dt != BF16 else B[:, at[0]:at[0] + cols]
        at[0] += 2 * cols if dt != BF16 else cols
        return v if dt == BF16 else v.bitcast(dt)

    X = carve(NB * D).rearrange("p (b f) -> p b f", b=NB)
    Hn = carve(NB * D).rearrange("p (b f) -> p b f", b=NB)
    tmp = carve(NB * D).rearrange("p (b f) -> p b f", b=NB)
    st = carve(4 * NB).rearrange("p (s b) -> p s b", s=4)
    srcI, dstI, shI = carve(G * T, I32), carve(G * T, I32), carve(G * T, I32)
    dg = carve(GE, I32)
    ramp = carve(KEYS, I32)
    ibase = carve(IC, I32)
    tri, shift = carve(P), carve(P)
    w40 = carve(MAXWIN, I32)
    gm = carve(16)
    nwB, dB = carve(P), carve(P)
    ends, jumps = carve(P), carve(P)
    past = carve(IC * G).rearrange("p (c g) -> p c g", c=IC)
    moved = past
    reach = past[:, 0, :]
    gi, bi, ifl = carve(IC), carve(IC), carve(IC)
    item = carve(IC * 2, I32).rearrange("p (c k) -> p c k", k=2)
    Wt = carve(3 * H * D).rearrange("p (w c) -> p w c", w=3)
    Wo = carve(H * D).rearrange("p (h o) -> p h o", h=H)
    WT = carve(3 * H * D).rearrange("p (w c) -> p w c", w=3)
    Mk = carve(H * D)
    HT = carve(NP)
    R3 = carve(NB * SP3 * H * D, BF16).rearrange("p (b s c) -> p b s c", b=NB, s=SP3)
    rest = carve(2 * 2 * 512).rearrange("p (r c) -> p r c", r=4)
    zero = carve(SP3 * H * D, BF16)
    edges = carve(G * 3 * T).rearrange("p (g k t) -> p g k t", g=G, k=3)
    assert at[0] <= NB * NP

    q = {n: sem("p_" + n) for n in (
        "x", "src", "dst", "dgrp", "w", "const", "own", "ownp", "var", "root", "wtp", "wt", "mk", "mkc",
        "nw", "cum", "items", "h", "htp", "ht", "r", "hi", "rem", "mid", "lo", "stored", "pads", "edges")}

    with nc.Block() as block:

        @block.sync
        def _(sp):
            sp.wait_ge(q["pads"], 3)
            sp.dma_start(X[:, 0:NB - 1, :], I["x"][0:(NB - 1) * P, :].rearrange("(b p) f -> p b f", p=P)).then_inc(q["x"], 16)
            sp.dma_start(X[0:LAST, NB - 1, :], I["x"][(NB - 1) * P:N, :]).then_inc(q["x"], 16)
            sp.dma_start(dg[0:G, :], I["dst"].rearrange("(g e) -> g e", g=G)).then_inc(q["dgrp"], 16)
            sp.dma_start(srcI[0:TP, :].rearrange("p (g t) -> p g t", t=T),
                         I["src"].rearrange("(g p t) -> p g t", p=TP, t=T)).then_inc(q["src"], 16)
            sp.dma_start(dstI[0:TP, :].rearrange("p (g t) -> p g t", t=T),
                         I["dst"].rearrange("(g p t) -> p g t", p=TP, t=T)).then_inc(q["dst"], 16)
            for k, w in enumerate((I["L0_gnn_Wq"], I["L0_gnn_Wk"], I["L0_gnn_Wv"])):
                sp.dma_start(Wt[0:D, k, :], w).then_inc(q["w"], 16)
            sp.dma_start(Wo[0:D, :, :], I["L0_gnn_Wo"].rearrange("(h c) o -> c h o", h=H)).then_inc(q["w"], 16)
            sp.wait_ge(q["items"], 1)
            sp.dma_start(S.items.rearrange("(p c) k -> p (c k)", p=P), item.rearrange("p c k -> p (c k)")).then_inc(q["stored"], 16)
            sp.wait_ge(q["h"], 1)
            sp.dma_start(S.h0.rearrange("(b p) f -> p b f", p=P), Hn).then_inc(q["stored"], 16)
            sp.dma_start(S.r3[NP:NPW].rearrange("n s c -> n (s c)"), zero[0:W, :]).then_inc(q["stored"], 16)
            sp.wait_ge(q["lo"], NB)
            sp.dma_start(S.r3[0:NP].rearrange("(b p) s c -> p b (s c)", p=P), R3.rearrange("p b s c -> p b (s c)")).then_inc(q["stored"], 16)
            sp.wait_ge(q["edges"], 1)
            sp.dma_start(S.edges.rearrange("g p k t -> p g (k t)"), edges[0:TP].rearrange("p g k t -> p g (k t)")).then_inc(q["stored"], 16)
            sp.wait_ge(q["stored"], 80)

        @block.gpsimd
        def _(g):
            own = Own(g, q["ownp"])
            own.did(g.memset(S.ident[:, :], 0.0))
            own.did(g.memset(tri, 1.0))
            own.did(g.memset(shift, 0.0))
            g.iota(ramp, pattern=[[1, KEYS]], base=0, channel_multiplier=0).then_inc(q["const"], 1)
            g.iota(ibase, pattern=[[1, IC]], base=0, channel_multiplier=IC).then_inc(q["const"], 1)
            g.iota(w40, pattern=[[W, MAXWIN]], base=W, channel_multiplier=0).then_inc(q["const"], 1)
            g.iota(S.third[:, :], pattern=[[0, 1]], base=0, channel_multiplier=171).then_inc(q["const"], 1)
            own.settle()
            g.affine_select(out=S.ident[:, :], in_=S.ident[:, :], compare_op=ALU.not_equal, fill=1.0, base=0,
                            pattern=[[-1, P]], channel_multiplier=1).then_inc(q["const"], 1)
            g.affine_select(out=tri, in_=tri, compare_op=ALU.is_ge, fill=0.0, base=0,
                            pattern=[[1, P]], channel_multiplier=-1).then_inc(q["const"], 1)
            own.step(g.affine_select(out=shift, in_=shift, compare_op=ALU.not_equal, fill=1.0, base=-1,
                                     pattern=[[-1, P]], channel_multiplier=1))
            own.step(g.affine_select(out=shift, in_=shift, compare_op=ALU.not_equal, fill=-1.0, base=0,
                                     pattern=[[-1, P]], channel_multiplier=1))
            g.memset(shift[:, G:G + 1], 0.0).then_inc(q["ownp"], 1)
            g.wait_ge(q["ownp"], 6)
            g.memset(shift[0:1, G:G + 1], 1.0).then_inc(q["const"], 1)

        @block.vector
        def _(v):
            own = Own(v, q["own"])
            v.memset(X[:, NB - 1, :], 0.0).then_inc(q["pads"], 1)
            v.memset(srcI, 0.0).then_inc(q["pads"], 1)
            v.memset(dstI, -4096.0).then_inc(q["pads"], 1)
            own.did(v.memset(zero, 0.0))
            own.did(v.memset(S.hpT[:, :], 0.0))
            v.wait_ge(q["const"], 7)
            own.did(v.tensor_copy(S.ramp[:, :], ramp))
            own.did(v.tensor_copy(S.identb[:, :], S.ident[:, :]))
            own.step(v.tensor_scalar(S.third[:, :], S.third[:, :], 9, None, ALU.logical_shift_right))
            own.did(v.tensor_copy(S.thirdf[:, :], S.third[:, :]))
            v.wait_ge(q["dgrp"], 16)
            own.did(v.tensor_reduce(gm[0:G, 0:1], dg[0:G, :], AX.X, ALU.max))
            own.step(v.tensor_reduce(gm[0:G, 1:2], dg[0:G, :], AX.X, ALU.min))
            own.step(v.tensor_tensor(gm[0:G, 2:3], gm[0:G, 0:1], gm[0:G, 1:2], ALU.subtract))
            own.step(v.tensor_scalar(reach[0:G, 0:MAXWIN], w40[0:G, :], gm[0:G, 2:3], None, ALU.is_le))
            own.step(v.tensor_reduce(gm[0:G, 3:4], reach[0:G, 0:MAXWIN], AX.X, ALU.add))
            own.step(v.tensor_scalar(gm[0:G, 4:5], gm[0:G, 3:4], 1.0, None, ALU.add))
            v.tensor_copy(nwB[0:G, :], gm[0:G, 4:5].to_broadcast([G, P])).then_inc(q["nw"], 1)
            v.wait_ge(q["cum"], 1)
            own.step(v.tensor_tensor(gm[0:G, 5:6], S.bank[1][0:G, 0:1], gm[0:G, 4:5], ALU.subtract))
            own.step(v.scalar_tensor_tensor(gm[0:G, 6:7], gm[0:G, 5:6], -float(W), gm[0:G, 1:2], ALU.mult, ALU.add))
            v.tensor_copy(dB[0:G, :], gm[0:G, 6:7].to_broadcast([G, P])).then_inc(q["nw"], 1)
            own.did(v.tensor_copy(ends[:, 0:G], S.bank[0][:, 0:G]))
            v.wait_ge(q["cum"], 2)
            own.step(v.tensor_copy(jumps[:, 0:G + 1], S.bank[2][:, 0:G + 1]))
            own.did(v.tensor_copy(S.count[:, 0:1], ends[0:1, G - 1:G]))
            own.step(v.scalar_tensor_tensor(jumps[:, G - 1:G], ends[:, G - 1:G], -float(W), jumps[:, G - 1:G], ALU.mult, ALU.add))
            own.step(v.tensor_scalar(jumps[:, G - 1:G], jumps[:, G - 1:G], float(NP - W), None, ALU.add))
            own.step(v.tensor_scalar(S.count[:, 2:3], S.count[:, 0:1], 1.0, None, ALU.add))
            own.step(v.tensor_scalar(S.count[:, 1:2], S.count[:, 2:3], 1, None, ALU.logical_shift_right))
            full = [P, IC, G]
            own.step(v.tensor_copy(ifl, ibase))
            own.step(v.tensor_tensor(past, over(ifl, full), ends[:, 0:G].unsqueeze(1).to_broadcast(full), ALU.is_ge))
            own.step(v.tensor_reduce(gi, past, AX.X, ALU.add))
            own.step(v.tensor_tensor(moved, past, jumps[:, 0:G].unsqueeze(1).to_broadcast(full), ALU.mult))
            own.step(v.tensor_reduce(bi, moved, AX.X, ALU.add))
            own.did(v.tensor_scalar(item[:, :, 0], gi, float(G - 1), None, ALU.min))
            own.step(v.tensor_scalar(bi, bi, jumps[:, G:G + 1], None, ALU.add))
            v.scalar_tensor_tensor(item[:, :, 1], ifl, float(W), bi, ALU.mult, ALU.add).then_inc(q["items"], 1)
            v.wait_ge(q["x"], 32)

            def act_turn():
                v.sem_inc(q["var"], 1)
                v.wait_ge(q["root"], 1)

            norm_steps(nc, own, X, Hn, tmp, st, D, True, act_turn)
            v.sem_inc(q["h"], 1)
            v.wait_ge(q["src"], 16)
            v.wait_ge(q["dst"], 16)
            own.step(v.tensor_scalar(shI, srcI, 7, None, ALU.arith_shift_right))
            own.did(v.tensor_copy(edges[:, :, 1, :], shI.rearrange("p (g t) -> p g t", t=T)))
            own.step(v.tensor_scalar(srcI, srcI, P - 1, None, ALU.bitwise_and))
            own.did(v.tensor_scalar(edges[:, :, 2, :], srcI.rearrange("p (g t) -> p g t", t=T), -1.0, None, ALU.mult))
            own.step(v.tensor_copy(edges[:, :, 0, :], dstI.rearrange("p (g t) -> p g t", t=T)))
            v.sem_inc(q["edges"], 1)
            for b in range(NB):
                r = S.bank[4 + b % 4][:, 0:H * D]
                v.wait_ge(q["hi"], b + 1)
                v.tensor_tensor(rest[:, b % 4, 0:H * D], r, R3[:, b, 0, :], ALU.subtract).then_inc(q["rem"], 1)
                v.wait_ge(q["mid"], b + 1)
                v.tensor_tensor(R3[:, b, 2, :], rest[:, b % 4, 0:H * D], R3[:, b, 1, :], ALU.subtract).then_inc(q["lo"], 1)

        @block.scalar
        def _(act):
            act.wait_ge(q["var"], 1)
            root(nc, st, NB).then_inc(q["root"], 1)
            for k in range(3):
                act.wait_ge(q["wtp"], k + 1)
                nc.scalar.activation(WT[0:D, k, :], S.bank[(3, 5, 6)[k]][0:D, 0:H * D],
                                     ACT.Copy, scale=D ** -0.5 if k == 0 else 1.0).then_inc(q["wt"], 1)
            act.wait_ge(q["mk"], 1)
            act.copy(Mk[0:D, :], S.bank[7][0:D, 0:H * D]).then_inc(q["mkc"], 1)
            act.copy(S.Mo[:, :], S.bank[4][0:D, 0:H * D]).then_inc(q["mkc"], 1)
            for b in range(NB + 1):
                if b < NB:
                    act.wait_ge(q["htp"], b + 1)
                    act.copy(HT[0:D, b * P:(b + 1) * P], S.bank[1 + b % 2][0:D, 0:P]).then_inc(q["ht"], 1)
                if b >= 1:
                    c = b - 1
                    act.wait_ge(q["r"], c + 1)
                    act.copy(R3[:, c, 0, :], S.bank[4 + c % 4][:, 0:H * D]).then_inc(q["hi"], 1)
                    act.wait_ge(q["rem"], c + 1)
                    act.copy(R3[:, c, 1, :], rest[:, c % 4, 0:H * D]).then_inc(q["mid"], 1)

        @block.tensor
        def _(pe):
            pe.wait_ge(q["const"], 7)
            pe.wait_ge(q["nw"], 1)
            pe.matmul(S.bank[0][:, 0:G], nwB[0:G, :], tri[0:G, 0:G], start=True, stop=True)
            pe.matmul(S.bank[1][0:G, 0:1], tri[0:G, 0:G], nwB[0:G, 0:1], start=True, stop=True).then_inc(q["cum"], 1)
            pe.wait_ge(q["nw"], 2)
            pe.matmul(S.bank[2][:, 0:G + 1], dB[0:G, :], shift[0:G, 0:G + 1], start=True, stop=True).then_inc(q["cum"], 1)
            pe.wait_ge(q["w"], 64)
            for k in range(3):
                o = S.bank[(3, 5, 6)[k]][0:D, 0:H * D]
                for h in range(H):
                    mm = pe.transpose(o[:, h * D:(h + 1) * D], Wt[0:D, k, h * D:(h + 1) * D], S.ident[0:D, 0:D])
                mm.then_inc(q["wtp"], 1)
            pe.wait_ge(q["wt"], 3)
            for h in range(H):
                c = slice(h * D, (h + 1) * D)
                pe.matmul(S.bank[7][0:D, c], WT[0:D, 1, c], WT[0:D, 0, c], start=True, stop=True)
                mm = pe.matmul(S.bank[4][0:D, c], WT[0:D, 2, c], Wo[0:D, h, :], start=True, stop=True)
            mm.then_inc(q["mk"], 1)
            pe.wait_ge(q["mkc"], 2)
            pe.wait_ge(q["h"], 1)
            for b in range(NB + 1):
                if b < NB:
                    if b >= 2:
                        pe.wait_ge(q["ht"], b - 1)
                    pe.transpose(S.bank[1 + b % 2][0:D, 0:P], Hn[:, b, :], S.ident[:, :]).then_inc(q["htp"], 1)
                if b >= 1:
                    c = b - 1
                    pe.wait_ge(q["ht"], c + 1)
                    if c >= 4:
                        pe.wait_ge(q["rem"], c - 3)
                    pe.matmul(S.bank[4 + c % 4][:, 0:H * D], HT[0:D, c * P:(c + 1) * P], Mk[0:D, :],
                              start=True, stop=True).then_inc(q["r"], 1)


def attend(nc, I, S, sb, sem):
    HT = T // 2
    spot = sb("spot", [P, 2, 2], I32)
    idx = sb("idx", [P, 2, T], I32)
    dstrow = sb("dstrow", [KW, GE], I32)
    rwin = sb("rwin", [KW, 2, H * D], BF16)
    hsrc = sb("hsrc", [P, 2, T, D], F32)
    there = sb("there", [KW, GE], BF16)
    lo = sb("lo", [P, 2, T, P], BF16)
    hot = sb("hot", [P, 4, KEYS], BF16)
    prod = sb("prod", [P, HT * H * D], F32)
    at = sb("at", [P, T, W], BF16)
    AO = sb("AO", [P, 2, HT, H, W], F32)
    edges = sb("edges", [P, 2, 3, T], F32)
    small = sb("small", [P, 6, T * H], F32)
    last = sb("last", [1, 1], I32)
    thr = sb("thr", [P, 1], F32)
    ones = sb("ones", [P, 1], F32)
    U = sb("U", [D, H * W], F32)
    dl, key, top = (small[0:TP, k, 0:T] for k in range(3))
    score, expo, attn = (small[0:TP, k, :] for k in range(3, 6))

    q = {n: sem("a_" + n) for n in (
        "spot0", "spot1", "edges0", "edges1", "idx0", "idx1", "rwin0", "rwin1", "dstrow", "zero", "pad", "spot_free", "window_free", 
        "there", "lo", "squares", "lo_free", "hot", "hot_free", "scores", "scores_free", "soft", "expo", "attn", "ao", "ao_free", "carrier",
        "idx_free", "counted", "count_free", "u", "u_free", "zeros", "proj", "proj_free", "own")}
    got = [[sem(f"a_got{s}{t}") for t in range(T)] for s in range(2)]
    STEPS = 9
    half = NB * NP // 2

    def pairs_of(eng):
        return eng.value_load(S.count[0:1, 1:2], min_val=1, max_val=-(-G * MAXWIN // 2))

    with nc.Block() as block:

        @block.sync
        def _(sp):
            sp.wait_ge(q["pad"], 1)
            n = pairs_of(sp)
            with sp.Fori(0, n) as j:
                for s in range(2):
                    i = j * 2 + s
                    g = sp.value_load(S.items[bass.ds(i, 1), 0:1], min_val=0, max_val=G - 1)
                    b = sp.value_load(S.items[bass.ds(i, 1), 1:2], min_val=0, max_val=NP - W)
                    sp.wait_ge(q["spot_free"], i + 1)
                    sp.dma_start(spot[:, s, :], S.items[bass.ds(i, 1), :].to_broadcast([P, 2])).then_inc(q[f"spot{s}"], 16)
                    sp.wait_ge(q["lo"], i + 1)
                    sp.dma_start(edges[0:TP, s, :, :], S.edges[bass.ds(g, 1)].rearrange("g p k t -> p (g k) t")).then_inc(q[f"edges{s}"], 16)
                    sp.wait_ge(q["idx_free"], i + 1)
                    sp.dma_start(idx[0:TP, s, :], I["src"][bass.ds(g * GE, GE)].rearrange("(p t) -> p t", t=T)).then_inc(q[f"idx{s}"], 16)
                    sp.wait_ge(q["window_free"], i + 1)
                    sp.dma_start(rwin[:, s, :], S.r3[bass.ds(b, W)].rearrange("n s c -> (n s) c")).then_inc(q[f"rwin{s}"], 16)
                    sp.wait_ge(q["there"], i + 1)
                    sp.dma_start(dstrow[:, :], I["dst"][bass.ds(g * GE, GE)].unsqueeze(0).to_broadcast([KW, GE])).then_inc(q["dstrow"], 16)
            g = sp.value_load(S.items[bass.ds(n * 2, 1), 0:1], min_val=0, max_val=G - 1)
            sp.wait_ge(q["spot_free"], n * 2 + 1)
            sp.dma_start(spot[:, 0, :], S.items[bass.ds(n * 2, 1), :].to_broadcast([P, 2])).then_inc(q["spot0"], 16)
            sp.wait_ge(q["lo"], n * 2 + 1)
            sp.dma_start(edges[0:TP, 0, :, :], S.edges[bass.ds(g, 1)].rearrange("g p k t -> p (g k) t")).then_inc(q["edges0"], 16)
            sp.wait_ge(q["there"], n * 2 + 1)
            sp.dma_start(dstrow[:, :], I["dst"][bass.ds(g * GE, GE)].unsqueeze(0).to_broadcast([KW, GE])).then_inc(q["dstrow"], 16)
            sp.wait_ge(q["idx_free"], n * 2 + 1)
            sp.dma_start(idx[0:TP, 0, :], I["src"][bass.ds(g * GE, GE)].rearrange("(p t) -> p t", t=T)).then_inc(q["idx0"], 16)

        @block.gpsimd
        def _(g):
            g.memset(idx[:, :, :], 0.0).then_inc(q["pad"], 1)
            g.memset(hsrc[:, 1, :, :], 0.0).then_inc(q["zeros"], 1)
            g.memset(AO[:, :, :, :, :], 0.0).then_inc(q["zeros"], 1)
            g.memset(ones[:, :], 1.0).then_inc(q["zeros"], 1)
            g.memset(S.A[:, half:2 * half].bitcast(F32), 0.0).then_inc(q["zero"], 1)
            g.sem_inc(q["ao"], 2)

            def gather(n, s, seen):
                g.wait_ge(q[f"idx{s}"], seen)
                for t in range(T):
                    if t % HT == 0:
                        g.wait_ge(q["ao_free"], 2 * n + t // HT + 1)
                        g.sem_inc(q["carrier"], 1)
                    g.indirect_dma_start(out=hsrc[:, s, t, :], out_offset=None, in_=S.h0[:, :],
                                         in_offset=bass.IndirectOffsetOnAxis(ap=idx[:, s, t:t + 1], axis=0)
                                         ).then_inc(got[s][t], 16)

            gather(0, 0, 16)
            shape = [TP, HT, H, W]
            n = pairs_of(g)
            with g.Fori(0, n) as j:
                for s in range(2):
                    i = j * 2 + s
                    gather(i + 1, 1 - s, j * 16 + 16 + 16 * s)
                    g.wait_ge(q["attn"], i + 1)
                    for hf in range(2):
                        t0 = hf * HT
                        g.tensor_tensor(AO[0:TP, hf, :, :, :], at[0:TP, t0:t0 + HT, :].unsqueeze(2).to_broadcast(shape),
                                        attn.rearrange("p (t h) -> p t h", h=H)[:, t0:t0 + HT, :].unsqueeze(3).to_broadcast(shape),
                                        ALU.mult).then_inc(q["ao"], 1)
            for t in range(T):
                g.wait_ge(got[0][t], n * 16 + 16)

        @block.vector
        def _(v):
            v.sem_inc(q["spot_free"], 2)
            v.sem_inc(q["there"], 1)
            v.sem_inc(q["scores_free"], 2)
            v.sem_inc(q["proj_free"], 1)
            v.sem_inc(q["count_free"], 2)
            v.sem_inc(q["idx_free"], 2)
            first = Own(v, q["own"])
            first.step(v.memset(last[:, :], 0.0))
            v.memset(S.A[:, 0:half].bitcast(F32), 0.0).then_inc(q["zero"], 1)
            v.wait_ge(q["zero"], 2)

            def place(own, n, s, seen):
                v.wait_ge(q[f"spot{s}"], seen)
                own.did(v.tensor_scalar(thr[0:KW, :], S.thirdf[0:KW, :], spot[0:KW, s, 1:2], None, ALU.add))
                v.wait_ge(q[f"edges{s}"], seen)
                own.settle()
                own.did(v.tensor_scalar(dl, edges[0:TP, s, 0, :], spot[0:TP, s, 1:2], None, ALU.subtract))
                v.wait_ge(q["window_free"], n + 2)
                v.wait_ge(q["dstrow"], n * 16 + 16)
                own.settle()
                v.tensor_scalar(there[:, :], dstrow[:, :], thr[0:KW, :], None, ALU.is_equal).then_inc(q["there"], 1)
                own.did(v.scalar_tensor_tensor(key, dl, float(NB), edges[0:TP, s, 1, :], ALU.mult, ALU.add))

            place(first, 0, 0, 16)
            with v.Fori(0, pairs_of(v)) as j:
                for s in range(2):
                    i = j * 2 + s
                    own = Own(v, q["own"], j * (2 * STEPS + 1) + s * STEPS + 4)
                    th = "p (t h) -> p t h"
                    four = [TP, HT, H, D]
                    s4, e4, a4 = (x.rearrange(th, h=H) for x in (score, expo, attn))

                    def keys(t0, t1):
                        for t in range(t0, t1):
                            v.wait_ge(q["hot_free"], T * i + t + 1)
                            v.tensor_scalar(hot[0:TP, t % 4, :], S.ramp[0:TP, :], key[:, t:t + 1], None,
                                            ALU.is_equal).then_inc(q["hot"], 1)

                    def products(hf):
                        v.wait_ge(q["scores"], 2 * i + hf + 1)
                        for t in range(HT):
                            v.wait_ge(got[s][HT * hf + t], j * 16 + 16)
                        v.tensor_tensor(prod[0:TP, :].rearrange("p (t h f) -> p t h f", t=HT, h=H),
                                        S.ps[0:TP, hf * 1024:(hf + 1) * 1024].rearrange("p (t h f) -> p t h f", t=HT, h=H),
                                        hsrc[0:TP, s, HT * hf:HT * (hf + 1), :].unsqueeze(2).to_broadcast(four),
                                        ALU.mult).then_inc(q["scores_free"], 1)

                    def sums(hf):
                        v.wait_ge(q["scores_free"], 2 * i + hf + 3)
                        return own.did(v.tensor_reduce(score[:, hf * HT * H:(hf + 1) * HT * H],
                                                       prod[0:TP, :].rearrange("p (c f) -> p c f", f=D), AX.X, ALU.add))

                    def add_counts(k):
                        part = S.A[:, :].rearrange("p (b n) -> p b n", b=NB)[:, :, bass.ds(b + k * (W // 2), W // 2)]
                        seen = S.ps[:, 2048 + 512 * k:2048 + 512 * k + KEYS // 2].rearrange("p (w b) -> p b w", b=NB)
                        v.tensor_tensor(part, part, seen, ALU.add).then_inc(q["count_free"], 1)

                    v.wait_ge(q["own"], own.base)
                    keys(0, 2)
                    b = v.value_load(spot[0:1, s, 1:2], min_val=0, max_val=NP - W)
                    if s == 0:
                        before, b0 = v.value_load(last[0:1, 0:1], min_val=0, max_val=NP - W), b
                    else:
                        before = b0
                        own.did(v.tensor_copy(last[:, :], spot[0:1, s, 1:2]))
                    products(0)
                    keys(2, 4)
                    sums(0)
                    keys(4, 6)
                    own.settle()
                    products(1)
                    v.sem_inc(q["idx_free"], 1)
                    keys(6, 8)
                    summed = sums(1)
                    v.wait_ge(q["ao"], 2 * i + 2)
                    own.did(v.tensor_tensor(at[0:TP, :, :], S.ramp[0:TP, 0:W].unsqueeze(1).to_broadcast([TP, T, W]),
                                            over(dl, [TP, T, W]), ALU.is_equal))
                    v.sem_inc(q["spot_free"], 1)
                    v.wait_ge(q["hot"], T * i + T)
                    place(own, i + 1, 1 - s, j * 16 + 16 + 16 * s)
                    topped = own.did(v.tensor_reduce(top, s4, AX.X, ALU.max))
                    v.wait_ge(q["counted"], i + 1)
                    add_counts(0)
                    own.settle(topped)
                    v.tensor_tensor(s4, s4, over(top, [TP, T, H]), ALU.subtract).then_inc(q["soft"], 1)
                    add_counts(1)
                    v.wait_ge(q["proj"], i + 2)
                    v.tensor_tensor(S.hpT[:, bass.ds(before, W)], S.hpT[:, bass.ds(before, W)], S.ps[0:D, 3584:3584 + W],
                                    ALU.add).then_inc(q["proj_free"], 1)
                    v.wait_ge(q["expo"], i + 1)
                    own.step(v.tensor_reduce(top, e4, AX.X, ALU.add))
                    own.step(v.reciprocal(top, top))
                    v.tensor_tensor(a4, e4, over(top, [TP, T, H]), ALU.mult).then_inc(q["attn"], 1)
                    assert own.n == STEPS + s, (own.n, s)
            n = pairs_of(v)
            b = v.value_load(last[0:1, 0:1], min_val=0, max_val=NP - W)
            v.wait_ge(q["proj"], n * 2 + 2)
            v.tensor_tensor(S.hpT[:, bass.ds(b, W)], S.hpT[:, bass.ds(b, W)], S.ps[0:D, 3584:3584 + W], ALU.add)

        @block.scalar
        def _(act):
            act.sem_inc(q["u_free"], 1)
            act.sem_inc(q["lo"], 2)

            act.wait_ge(q["zeros"], 3)

            def bring_sums(n):
                act.wait_ge(q["u"], n + 1)
                act.wait_ge(q["proj"], n + 1)
                act.copy(U[:, :], S.ps[0:D, 3072:3072 + H * W]).then_inc(q["u_free"], 1)

            def rows(n, s, seen):
                act.wait_ge(q[f"edges{s}"], seen)
                act.wait_ge(q["lo_free"], n + 1)
                for t in range(T):
                    op = nc.scalar.activation(lo[0:TP, s, t, :], S.ramp[0:TP, 0:P], ACT.Square, bias=edges[0:TP, s, 2, t:t + 1])
                op.then_inc(q["squares"], 1)
                act.wait_ge(q["squares"], n + 1)
                nc.scalar.activation(lo[0:TP, s, :, :], lo[0:TP, s, :, :], ACT.Relu, bias=ones[0:TP, :], scale=-1.0).then_inc(q["lo"], 1)

            rows(0, 0, 16)
            with act.Fori(0, pairs_of(act)) as j:
                for s in range(2):
                    i = j * 2 + s
                    bring_sums(i)
                    rows(i + 1, 1 - s, j * 16 + 16 + 16 * s)
                    act.wait_ge(q["soft"], i + 1)
                    nc.scalar.activation(expo, score, ACT.Exp).then_inc(q["expo"], 1)
            bring_sums(pairs_of(act) * 2)

        @block.tensor
        def _(pe):
            pe.sem_inc(q["window_free"], 2)
            pe.sem_inc(q["lo_free"], 2)
            pe.sem_inc(q["hot_free"], 4)
            pe.sem_inc(q["ao_free"], 2)
            pe.sem_inc(q["proj"], 1)
            pe.wait_ge(q["zeros"], 3)

            def weigh(n, hf, s):
                if hf == 0:
                    pe.wait_ge(q["u_free"], n + 1)
                pe.wait_ge(q["ao"], 2 * n + hf + 1)
                for t in range(hf * HT, hf * HT + HT):
                    mm = pe.matmul(S.ps[0:D, 3072:3072 + H * W], hsrc[0:TP, s, t, :],
                                   AO[0:TP, hf, t % HT, :, :].rearrange("p h w -> p (h w)"),
                                   start=(t == 0), stop=(t == T - 1))
                mm.then_inc(q["ao_free"], 1)
                if hf == 1:
                    pe.wait_ge(q["ao_free"], 2 * n + 4)
                    pe.sem_inc(q["u"], 1)

            def project(n):
                pe.wait_ge(q["u_free"], n + 2)
                pe.wait_ge(q["proj_free"], n + 1)
                pe.sem_inc(q["carrier"], 1)
                for h in range(H):
                    mm = pe.matmul(S.ps[0:D, 3584:3584 + W], S.Mo[:, h * D:(h + 1) * D], U[:, h * W:(h + 1) * W],
                                   start=(h == 0), stop=(h == H - 1))
                mm.then_inc(q["proj"], 1)

            n = pairs_of(pe)
            with pe.Fori(0, n) as j:
                for s in range(2):
                    i = j * 2 + s
                    pe.wait_ge(q["there"], i + 2)
                    pe.wait_ge(q[f"rwin{s}"], j * 16 + 16)
                    for t in range(T):
                        if t % HT == 0:
                            pe.wait_ge(q["scores_free"], 2 * i + t // HT + 1)
                        mm = pe.matmul(S.ps[0:TP, t * 256:(t + 1) * 256],
                                       there[:, :].rearrange("k (p t) -> k t p", t=T)[:, t, :], rwin[:, s, :],
                                       start=True, stop=True, skip_group_check=True)
                        if t % HT == HT - 1:
                            mm.then_inc(q["scores"], 1)
                    pe.wait_ge(q["lo"], i + 3)
                    pe.wait_ge(q["count_free"], 2 * i + 2)
                    for t in range(T):
                        pe.wait_ge(q["hot"], T * i + t + 1)
                        pe.matmul(S.ps[:, 2048:2048 + 500], lo[0:TP, s, t, :], hot[0:TP, t % 4, 0:500],
                                  start=(t == 0), stop=(t == T - 1))
                        pe.matmul(S.ps[:, 2560:2560 + 500], lo[0:TP, s, t, :], hot[0:TP, t % 4, 500:1000],
                                  start=(t == 0), stop=(t == T - 1)).then_inc(q["hot_free"], 1)
                        if t == 1:
                            pe.wait_ge(q["scores"], 2 * i + 2)
                            pe.sem_inc(q["window_free"], 1)
                        if t in (1, 3):
                            weigh(i, t // 2, 1 - s)
                    pe.wait_ge(q["hot_free"], T * i + T + 4)
                    pe.sem_inc(q["lo_free"], 1)
                    pe.sem_inc(q["counted"], 1)
                    project(i)
            for hf in range(2):
                weigh(n * 2, hf, 1)
            project(n * 2)


def turn(nc, I, S, sb, sem):
    f3 = [P, NB, D]
    X, Hn, Y, tmp = (sb(n, f3, F32)[:, :, :] for n in ("t_x", "t_h", "t_y", "t_tmp"))
    st = sb("t_st", [P, 4, NB], F32)[:, :, :]
    deg = sb("t_deg", [P, 4, NB], F32)
    gam = sb("t_gam", [P, 2, D], F32)
    ones = sb("t_ones", [P, 1], BF16)
    q = {n: sem("t_" + n) for n in (
        "x", "h", "gam", "own", "pair", "back_v", "back_a", "hpt", "hpt_free", "one", "var", "root", "turned",
        "rdeg", "rootd", "store", "stored", "var2", "root2", "hdone", "pads", "all", "row", "rowc")}
    groups = [(i, j, min(4, NB - j)) for i in range(NB) for j in range(i + 1, NB, 4)]

    def block_at(r, c):
        return S.A[:, r * NP + c * P:r * NP + (c + 1) * P]

    with nc.Block() as block:

        @block.sync
        def _(sp):
            sp.dma_start(Hn, S.h0.rearrange("(b p) f -> p b f", p=P)).then_inc(q["h"], 16)
            sp.wait_ge(q["pads"], 1)
            sp.dma_start(X[:, 0:NB - 1, :], I["x"][0:(NB - 1) * P, :].rearrange("(b p) f -> p b f", p=P)).then_inc(q["x"], 16)
            sp.dma_start(X[0:LAST, NB - 1, :], I["x"][(NB - 1) * P:N, :]).then_inc(q["x"], 16)
            sp.dma_start(gam[:, 0, :], I["L0_gnn_gamma"].unsqueeze(0).to_broadcast([P, D])).then_inc(q["gam"], 16)
            sp.dma_start(gam[:, 1, :], I["L0_gnn_beta"].unsqueeze(0).to_broadcast([P, D])).then_inc(q["gam"], 16)
            sp.wait_ge(q["store"], 1)
            sp.dma_start(S.xs.rearrange("(p b) f -> p b f", p=P), X).then_inc(q["stored"], 16)
            sp.wait_ge(q["hdone"], 1)
            sp.dma_start(S.hs.rearrange("(p b) f -> p b f", p=P), Hn).then_inc(q["stored"], 16)
            sp.wait_ge(q["stored"], 32)

        @block.tensor
        def _(pe):
            for b in range(NB):
                if b % 8 == 0 and b >= 16:
                    pe.wait_ge(q["hpt_free"], b // 8 - 1)
                mm = pe.transpose(S.ps[:, 3072 + 512 * (b // 8 % 2) + D * (b % 8):3072 + 512 * (b // 8 % 2) + D * (b % 8) + D],
                                  S.hpT[:, b * P:(b + 1) * P], S.ident[0:D, 0:D])
                if b % 8 == 7 or b == NB - 1:
                    mm.then_inc(q["hpt"], 1)
            for n, (i, j, c) in enumerate(groups):
                if n >= 3:
                    pe.wait_ge(q["back_v"], n - 2)
                    pe.wait_ge(q["back_a"], n - 2)
                for m in range(c):
                    pe.matmul(S.bank[n % 3 * 2][:, m * P:(m + 1) * P], block_at(i, j + m), S.identb[:, :], start=True, stop=True)
                for m in range(c):
                    mm = pe.matmul(S.bank[n % 3 * 2 + 1][:, m * P:(m + 1) * P], block_at(j + m, i), S.identb[:, :], start=True, stop=True)
                mm.then_inc(q["pair"], 1)
            pe.wait_ge(q["back_v"], len(groups))
            pe.wait_ge(q["back_a"], len(groups))
            for n in range(7):
                for b in range(4 * n, min(4 * n + 4, NB)):
                    if b % 4 == 0 and n >= 6:
                        pe.wait_ge(q["one"], n - 5)
                    mm = pe.matmul(S.bank[n % 6][:, (b % 4) * P:(b % 4 + 1) * P], S.A[:, b * (NP + P):b * (NP + P) + P],
                                   S.identb[:, :], start=True, stop=True)
                mm.then_inc(q["all"], 1)
            pe.wait_ge(q["one"], 7)
            for n in range(7):
                w = min(512, NP - 512 * n)
                if n == 6:
                    pe.wait_ge(q["rowc"], 1)
                for j in range(NB):
                    mm = pe.matmul(S.bank[n % 6][0:1, 0:w], ones[:, :], S.A[:, j * NP + 512 * n:j * NP + 512 * n + w],
                                   start=(j == 0), stop=(j == NB - 1))
                mm.then_inc(q["row"], 1)
            pe.wait_ge(q["rowc"], 7)
            for b in range(NB):
                mm = pe.transpose(S.bank[7][:, b:b + 1], S.hpT[0:1, b * P:(b + 1) * P], S.ident[0:1, 0:1])
            mm.then_inc(q["turned"], 1)

        @block.gpsimd
        def _(g):
            nc.clear_and_free_semaphores(S.done)

        @block.scalar
        def _(act):
            for n, (i, j, c) in enumerate(groups):
                act.wait_ge(q["pair"], n + 1)
                act.copy(S.A[:, i * NP + j * P:i * NP + (j + c) * P], S.bank[n % 3 * 2 + 1][:, 0:c * P]).then_inc(q["back_a"], 1)
            act.wait_ge(q["var"], 1)
            root(nc, st, NB).then_inc(q["root"], 1)
            act.wait_ge(q["var2"], 1)
            root(nc, st, NB).then_inc(q["root2"], 1)
            for n in range(7):
                w = min(512, NP - 512 * n)
                act.wait_ge(q["row"], n + 1)
                act.copy(S.hpT[0:1, 512 * n:512 * n + w], S.bank[n % 6][0:1, 0:w]).then_inc(q["rowc"], 1)
            act.wait_ge(q["rdeg"], 1)
            nc.scalar.activation(deg[:, 2, :], deg[:, 1, :], ACT.Sqrt).then_inc(q["rootd"], 1)

        @block.vector
        def _(v):
            own = Own(v, q["own"])
            v.memset(X[:, NB - 1, :], 0.0).then_inc(q["pads"], 1)
            own.did(v.memset(ones[:, :], 1.0))
            v.wait_ge(q["h"], 16)
            for n in range(4):
                v.wait_ge(q["hpt"], n + 1)
                c = min(8, NB - 8 * n)
                v.tensor_tensor(Y[:, 8 * n:8 * n + c, :], Hn[:, 8 * n:8 * n + c, :],
                                S.bank[6 + n % 2][:, 0:c * D].rearrange("p (b f) -> p b f", f=D), ALU.add).then_inc(q["hpt_free"], 1)
            v.wait_ge(q["hpt_free"], 4)
            for n, (i, j, c) in enumerate(groups):
                v.wait_ge(q["pair"], n + 1)
                v.tensor_copy(S.A[:, :].rearrange("p (b n) -> p b n", b=NB)[:, j:j + c, i * P:(i + 1) * P],
                              S.bank[n % 3 * 2][:, 0:c * P].rearrange("p (b n) -> p b n", n=P)).then_inc(q["back_v"], 1)
            for n in range(7):
                v.wait_ge(q["all"], n + 1)
                for b in range(4 * n, min(4 * n + 4, NB)):
                    op = v.tensor_copy(S.A[:, b * (NP + P):b * (NP + P) + P], S.bank[n % 6][:, (b % 4) * P:(b % 4 + 1) * P])
                op.then_inc(q["one"], 1)
            v.wait_ge(q["one"], 7)

            def turn_of(var, done):
                def f():
                    v.sem_inc(q[var], 1)
                    v.wait_ge(q[done], 1)
                return f

            norm_steps(nc, own, Y, Hn, tmp, st, D, False, turn_of("var", "root"))
            v.wait_ge(q["gam"], 32)
            v.wait_ge(q["x"], 32)
            row = lambda k: gam[:, k, :].unsqueeze(1).to_broadcast(f3)
            own.step(v.tensor_tensor(tmp, tmp, row(0), ALU.mult))
            own.step(v.tensor_tensor(tmp, tmp, row(1), ALU.add))
            own.step(v.tensor_tensor(X, X, tmp, ALU.add))
            v.sem_inc(q["store"], 1)
            norm_steps(nc, own, X, Hn, tmp, st, D, True, turn_of("var2", "root2"))
            v.sem_inc(q["hdone"], 1)
            tb = Y.rearrange("p b f -> p (b f)").bitcast(BF16).rearrange("p (b n) -> p b n", n=P)
            wide = [P, NB - 1, P]
            own.did(v.tensor_tensor(tb[:, 0:NB - 1, :], S.A[:, 0:(NB - 1) * (NP + P)].rearrange("p (b n) -> p b n", n=NP + P)[:, :, 0:P],
                                    S.identb[:, :].unsqueeze(1).to_broadcast(wide), ALU.mult))
            own.step(v.tensor_tensor(tb[:, NB - 1, :], S.A[:, (NB - 1) * (NP + P):NB * NP], S.identb[:, :], ALU.mult))
            own.step(v.tensor_reduce(deg[:, 3, :], tb, AX.X, ALU.add))
            v.wait_ge(q["turned"], 1)
            own.step(v.tensor_tensor(deg[:, 0, :], S.bank[7][:, 0:NB], deg[:, 3, :], ALU.subtract))
            own.step(v.tensor_scalar(deg[:, 1, :], deg[:, 0, :], 1.0, None, ALU.max))
            own.step(v.reciprocal(deg[:, 1, :], deg[:, 1, :]))
            v.sem_inc(q["rdeg"], 1)
            own.step(v.tensor_scalar(deg[:, 0, :], deg[:, 0, :], 0.0, None, ALU.is_gt))
            v.wait_ge(q["rootd"], 1)
            own.step(v.tensor_tensor(S.dinv[:, 0, :], deg[:, 2, :], deg[:, 0, :], ALU.mult))
            own.did(v.tensor_scalar(S.dinv[:, 1, :], S.dinv[:, 0, :], 2.0, None, ALU.mult))
            own.step(v.tensor_tensor(S.dinv[:, 2, :], S.dinv[:, 0, :], deg[:, 3, :], ALU.mult))


def split3(nc, own, src, parts):
    v = nc.vector
    own.step(v.tensor_copy(parts[:, :, 0, :], src))
    own.step(v.tensor_tensor(src, src, parts[:, :, 0, :], ALU.subtract))
    own.step(v.tensor_copy(parts[:, :, 1, :], src))
    own.step(v.tensor_tensor(parts[:, :, 2, :], src, parts[:, :, 1, :], ALU.subtract))


def linear_pe(nc, S, q, srcs, XT, weights, width):
    pe = nc.tensor
    K = srcs[0].shape[2]
    for b in range(NB + 1):
        if b < NB:
            if b >= 2:
                pe.wait_ge(q["lin_t"], b - 1)
            for k, x in enumerate(srcs):
                mm = pe.transpose(S.bank[6 + b % 2][0:K, k * P:(k + 1) * P], x[:, b, :], S.ident[:, :])
            mm.then_inc(q["lin_tp"], 1)
        if b >= 1:
            c = b - 1
            pe.wait_ge(q["lin_t"], c + 1)
            if c >= 2:
                pe.wait_ge(q["lin_used"], c - 1)
            for k in range(len(srcs)):
                mm = pe.matmul(S.bank[4 + c % 2][:, 0:width], XT[0:K, c % 2, k * P:(k + 1) * P], weights[k],
                               start=(k == 0), stop=(k == len(srcs) - 1))
            mm.then_inc(q["lin"], 1)


def linear_act(nc, S, q, n, K, XT):
    act = nc.scalar
    for b in range(NB):
        act.wait_ge(q["lin_tp"], b + 1)
        if b >= 2:
            act.wait_ge(q["lin"], b - 1)
        act.copy(XT[0:K, b % 2, 0:n * P], S.bank[6 + b % 2][0:K, 0:n * P]).then_inc(q["lin_t"], 1)


LINEAR = ("lin_t", "lin_tp", "lin", "lin_used")


def chebyshev(nc, I, S, sb, sem):
    f3 = [P, NB, D]
    X, T0, T1, T2, tmp = (sb(n, f3, F32)[:, :, :] for n in ("c_x", "c_0", "c_1", "c_2", "c_tmp"))
    parts = sb("c_parts", [P, NB, SP3, D], BF16)[:, :, :, :]
    zeros = sb("c_zeros", [P, 2 * D], F32)
    red = sb("c_red", [P, 2, D], F32)
    XT = sb("c_XT", [D, 2, 3 * P], F32)
    Wc = sb("c_w", [D, 2, 3, D], F32)
    bias = sb("c_b", [P, 2, D], F32)
    st = sb("c_st", [P, 4, NB], F32)[:, :, :]
    UN = 5
    assert NB % UN == 0
    q = {n: sem("c_" + n) for n in ("x", "h", "w", "own", "ready", "var", "root", "xdone", "hdone", "stored", "blk", "zeros")}
    props = [{n: sem(f"c_{n}{k}") for n in ("prod", "free", "own")} for k in range(4)]
    lins = [{n: sem(f"c_{n}{k}") for n in LINEAR} for k in range(2)]

    with nc.Block() as block:

        @block.sync
        def _(sp):
            sp.dma_start(T0, S.hs.rearrange("(p b) f -> p b f", p=P)).then_inc(q["h"], 16)
            sp.dma_start(X, S.xs.rearrange("(p b) f -> p b f", p=P)).then_inc(q["x"], 16)
            for k, (w, b) in enumerate(((I["L1_gnn_W0"], I["L1_gnn_b0"]), (I["L1_gnn_W1"], I["L1_gnn_b1"]))):
                sp.dma_start(Wc[:, k, :, :], w.rearrange("k i o -> i k o")).then_inc(q["w"], 16)
                sp.dma_start(bias[:, k, :], b.unsqueeze(0).to_broadcast([P, D])).then_inc(q["w"], 16)
            sp.wait_ge(q["zeros"], 1)
            for a in range(NACC):
                sp.dma_start(S.acc[a].rearrange("(p b) f -> p b f", p=P),
                             zeros[:, 0:D].unsqueeze(1).to_broadcast([P, ACCR // P, D])).then_inc(q["stored"], 16)
            sp.wait_ge(q["xdone"], 1)
            sp.dma_start(S.x2.rearrange("(p b) f -> p b f", p=P), X).then_inc(q["stored"], 16)
            sp.wait_ge(q["hdone"], 1)
            sp.dma_start(S.h2.rearrange("(p b) f -> p b f", p=P), T0).then_inc(q["stored"], 16)
            sp.dma_start(S.h3[0:NP].rearrange("(b p) s f -> p b (s f)", p=P), parts.rearrange("p b s f -> p b (s f)")).then_inc(q["stored"], 16)
            sp.dma_start(S.h3[NP:NPW].rearrange("n s f -> n (s f)"), zeros[0:W, :].bitcast(BF16)[:, 0:SP3 * D]).then_inc(q["stored"], 16)
            sp.wait_ge(q["stored"], 64 + 16 * NACC)

        @block.tensor
        def _(pe):
            for c in range(2):
                for k in range(2):
                    p = props[2 * c + k]
                    pe.wait_ge(q["ready"], 2 * c + k + 1)
                    with pe.Fori(0, NB // UN) as i:
                        for m in range(UN):
                            pe.wait_ge(p["free"], i * UN + m + 1)
                            for j in range(NB):
                                mm = pe.matmul(S.bank[m][:, 0:SP3 * D], S.A[:, bass.ds(i * (UN * P) + (j * NP + m * P), P)],
                                               parts[:, j, :, :].rearrange("p s f -> p (s f)"), start=(j == 0), stop=(j == NB - 1))
                            mm.then_inc(p["prod"], 1)
                pe.wait_ge(q["blk"], c + 1)
                pe.wait_ge(q["w"], 64)
                linear_pe(nc, S, lins[c], [T0, T1, T2], XT, [Wc[:, c, k, :] for k in range(3)], D)

        @block.scalar
        def _(act):
            for c in range(2):
                linear_act(nc, S, lins[c], 3, D, XT)
            act.wait_ge(q["var"], 1)
            root(nc, st, NB).then_inc(q["root"], 1)

        @block.vector
        def _(v):
            own = Own(v, q["own"])
            v.memset(zeros[:, :], 0.0).then_inc(q["zeros"], 1)
            v.wait_ge(q["h"], 16)
            for c in range(2):
                for k, (src, out) in enumerate(((T0, T1), (T1, T2))):
                    p = props[2 * c + k]
                    v.sem_inc(p["free"], UN)
                    own.step(v.tensor_tensor(tmp, src, over(S.dinv[:, 0, :], f3), ALU.mult))
                    split3(nc, own, tmp, parts)
                    v.sem_inc(q["ready"], 1)
                    sf = src.rearrange("p b f -> p (b f)")
                    of = out.rearrange("p b f -> p (b f)")
                    with v.Fori(0, NB // UN) as i:
                        mine = Own(v, p["own"], i * (UN * 3))
                        for m in range(UN):
                            b = i * UN + m
                            cols = bass.ds(i * (UN * D) + m * D, D)
                            v.wait_ge(p["prod"], b + 1)
                            mine.step(v.tensor_reduce(red[:, m % 2, :], S.bank[m][:, 0:SP3 * D].rearrange("p (s f) -> p f s", s=SP3),
                                                      AX.X, ALU.add))
                            v.sem_inc(p["free"], 1)
                            mine.step(v.scalar_tensor_tensor(red[:, m % 2, :], sf[:, cols], S.dinv[:, 2, bass.ds(b, 1)],
                                                             red[:, m % 2, :], ALU.mult, ALU.subtract))
                            if k == 0:
                                mine.step(v.tensor_scalar(of[:, cols], red[:, m % 2, :], S.dinv[:, 0, bass.ds(b, 1)], None, ALU.mult))
                            else:
                                mine.step(v.scalar_tensor_tensor(of[:, cols], red[:, m % 2, :], S.dinv[:, 1, bass.ds(b, 1)],
                                                                 T0.rearrange("p b f -> p (b f)")[:, cols], ALU.mult, ALU.subtract))
                        assert mine.n == UN * 3
                v.sem_inc(q["blk"], 1)
                v.wait_ge(q["w"], 64)
                for b in range(NB):
                    v.wait_ge(lins[c]["lin"], b + 1)
                    own.step(v.tensor_tensor(T0[:, b, :], S.bank[4 + b % 2][:, 0:D], bias[:, c, :], ALU.add))
                    v.sem_inc(lins[c]["lin_used"], 1)
                    own.step(v.tensor_scalar(T0[:, b, :], T0[:, b, :], 0.0, None, ALU.max))
            v.wait_ge(q["x"], 16)
            own.step(v.tensor_tensor(X, X, T0, ALU.add))
            v.sem_inc(q["xdone"], 1)

            def act_turn():
                v.sem_inc(q["var"], 1)
                v.wait_ge(q["root"], 1)

            norm_steps(nc, own, X, T0, tmp, st, D, True, act_turn)
            own.step(v.tensor_copy(tmp, T0))
            split3(nc, own, tmp, parts)
            v.sem_inc(q["hdone"], 1)


def messages(nc, I, S, sb, sem):
    spot = sb("m_spot", [P, 2, 2], I32)
    scol = sb("m_scol", [P, 2, T], I32)
    dcol = sb("m_dcol", [P, 2, T], I32)
    dstrow = sb("m_dstrow", [KW, GE], I32)
    srcrow = sb("m_srcrow", [TP, GE], I32)
    hwin = sb("m_hwin", [KW, 2, D], BF16)
    feat = sb("m_feat", [TP, 2, T, D], F32)
    there = sb("m_there", [KW, 2, GE], BF16)
    same = sb("m_same", [TP, 2, T, TP], F32)
    before = sb("m_before", [P, TP], F32)
    earlier = sb("m_earlier", [TP, T, TP], F32)
    xin = sb("m_xin", [TP, T, D], F32)
    msg = sb("m_msg", [TP, 2, T, D], F32)
    total = sb("m_total", [P, 2, T, D], F32)
    to = sb("m_to", [P, 2, T], I32)
    small = sb("m_small", [P, 4, T], F32)
    spare = sb("m_spare", [P, 1], F32)
    sparei = sb("m_sparei", [P, T], I32)
    thr = sb("m_thr", [P, 1], F32)
    dl, cnt, gap, ge0 = (small[0:TP, k, :] for k in range(4))
    home = sb("m_home", [P, 3, T], I32)
    valid = sb("m_valid", [TP, 2, T], F32)

    q = {n: sem("m_" + n) for n in (
        "spot0", "spot1", "scol0", "scol1", "dcol0", "dcol1", "hwin0", "hwin1", "feat0", "feat1", "dstrow", "srcrow",
        "cols_free", "dstrow_free", "srcrow_free", "window_free", "feat_free", "there", "near", "near_free", "x", "x_free",
        "msg", "msg_free", "same", "same_free", "sum", "sum_free", "total", "total_free", "to", "own", "carrier", "const",
        "const2")}
    added = [sem(f"m_added{a}") for a in range(NACC)]
    STEPS = 16

    def pairs_of(eng):
        return eng.value_load(S.count[0:1, 1:2], min_val=1, max_val=-(-G * MAXWIN // 2))

    with nc.Block() as block:

        @block.sync
        def _(sp):
            with sp.Fori(0, pairs_of(sp)) as j:
                for s in range(2):
                    i = j * 2 + s
                    g = sp.value_load(S.items[bass.ds(i, 1), 0:1], min_val=0, max_val=G - 1)
                    b = sp.value_load(S.items[bass.ds(i, 1), 1:2], min_val=0, max_val=NP - W)
                    sp.wait_ge(q["cols_free"], i + 1)
                    sp.dma_start(spot[:, s, :], S.items[bass.ds(i, 1), :].to_broadcast([P, 2])).then_inc(q[f"spot{s}"], 16)
                    sp.dma_start(dcol[0:TP, s, :], I["dst"][bass.ds(g * GE, GE)].rearrange("(p t) -> p t", t=T)).then_inc(q[f"dcol{s}"], 16)
                    sp.dma_start(scol[0:TP, s, :], I["src"][bass.ds(g * GE, GE)].rearrange("(p t) -> p t", t=T)).then_inc(q[f"scol{s}"], 16)
                    sp.wait_ge(q["window_free"], i + 1)
                    sp.dma_start(hwin[:, s, :], S.h3[bass.ds(b, W)].rearrange("n s f -> (n s) f")).then_inc(q[f"hwin{s}"], 16)
                    sp.wait_ge(q["feat_free"], i + 1)
                    sp.dma_start(feat[:, s, :, :], I["edge_attr_64"][bass.ds(g * GE, GE), :].rearrange("(p t) f -> p t f", t=T)).then_inc(q[f"feat{s}"], 16)
                    sp.wait_ge(q["dstrow_free"], i + 1)
                    sp.dma_start(dstrow[:, :], I["dst"][bass.ds(g * GE, GE)].unsqueeze(0).to_broadcast([KW, GE])).then_inc(q["dstrow"], 16)
                    sp.wait_ge(q["srcrow_free"], i + 1)
                    sp.dma_start(srcrow[:, :], I["src"][bass.ds(g * GE, GE)].unsqueeze(0).to_broadcast([TP, GE])).then_inc(q["srcrow"], 16)

        @block.gpsimd
        def _(g):
            g.iota(sparei[:, :], pattern=[[0, T]], base=NP, channel_multiplier=1).then_inc(q["const"], 1)
            g.memset(total[:, :, :, :], 0.0).then_inc(q["const"], 1)
            g.memset(before[:, :], 1.0).then_inc(q["const"], 1)
            g.wait_ge(q["const"], 3)
            g.affine_select(out=before[:, :], in_=before[:, :], compare_op=ALU.is_gt, fill=0.0, base=0,
                            pattern=[[-1, TP]], channel_multiplier=1).then_inc(q["const2"], 1)
            for a in range(NACC):
                g.indirect_dma_start(out=S.acc[a], out_offset=bass.IndirectOffsetOnAxis(ap=sparei[:, 0:1], axis=0),
                                     in_=total[:, 0, 0, :], in_offset=None, compute_op=ALU.add).then_inc(added[a], 16)
            for a in range(NACC):
                g.wait_ge(added[a], 16)
            g.sem_inc(q["total_free"], 1)
            n = pairs_of(g)
            with g.Fori(0, n) as j:
                for s in range(2):
                    i = j * 2 + s
                    g.wait_ge(q["total"], i + 1)
                    g.wait_ge(q["to"], i + 1)
                    for t in range(T):
                        if t == NACC:
                            g.sem_inc(q["total_free"], 1)
                        g.wait_ge(added[t % NACC], i * (16 * T // NACC) + 16 + 16 * (t // NACC))
                        g.sem_inc(q["carrier"], 1)
                        g.indirect_dma_start(out=S.acc[t % NACC], out_offset=bass.IndirectOffsetOnAxis(ap=to[:, s, t:t + 1], axis=0),
                                             in_=total[:, s, t, :], in_offset=None, compute_op=ALU.add).then_inc(added[t % NACC], 16)
            for a in range(NACC):
                g.wait_ge(added[a], n * (2 * 16 * T // NACC) + 16)
            g.sem_inc(q["carrier"], 1)

        @block.vector
        def _(v):
            for n, k in (("cols_free", 2), ("feat_free", 2), ("dstrow_free", 1), ("srcrow_free", 1), ("near_free", 2)):
                v.sem_inc(q[n], k)
            v.wait_ge(q["const"], 3)
            first = Own(v, q["own"])
            first.did(v.tensor_copy(spare[:, :], sparei[:, 0:1]))
            first.did(v.tensor_copy(to[:, :, :], sparei[:, :].unsqueeze(1).to_broadcast([P, 2, T])))
            v.wait_ge(q["const2"], 1)
            with v.Fori(0, pairs_of(v)) as j:
                for s in range(2):
                    i = j * 2 + s
                    own = Own(v, q["own"], i * STEPS + 2)
                    v.wait_ge(q[f"spot{s}"], j * 16 + 16)
                    own.did(v.tensor_scalar(thr[0:KW, :], S.thirdf[0:KW, :], spot[0:KW, s, 1:2], None, ALU.add))
                    v.wait_ge(q[f"dcol{s}"], j * 16 + 16)
                    own.step(v.tensor_scalar(dl, dcol[0:TP, s, :], spot[0:TP, s, 1:2], None, ALU.subtract))
                    own.step(v.tensor_scalar(ge0, dl, 0.0, None, ALU.is_ge))
                    v.wait_ge(q["msg_free"], i + 1)
                    own.did(v.scalar_tensor_tensor(valid[:, s, :], dl, float(W), ge0, ALU.is_lt, ALU.mult))
                    v.wait_ge(q["window_free"], i + 1)
                    v.wait_ge(q["dstrow"], i * 16 + 16)
                    own.step(v.tensor_scalar(there[:, s, :], dstrow[:, :], thr[0:KW, :], None, ALU.is_equal))
                    v.sem_inc(q["dstrow_free"], 1)
                    v.sem_inc(q["there"], 1)
                    v.wait_ge(q[f"scol{s}"], j * 16 + 16)
                    v.wait_ge(q["srcrow"], i * 16 + 16)
                    v.wait_ge(q["same_free"], i + 1)
                    full = [TP, T, TP]
                    own.step(v.tensor_tensor(same[:, s, :, :], srcrow[:, :].rearrange("k (p t) -> k t p", t=T),
                                             over(scol[0:TP, s, :], full), ALU.is_equal))
                    v.sem_inc(q["srcrow_free"], 1)
                    v.sem_inc(q["same"], 1)
                    own.step(v.tensor_tensor(earlier[:, :, :], same[:, s, :, :], before[0:TP, :].unsqueeze(1).to_broadcast(full), ALU.mult))
                    own.step(v.tensor_reduce(cnt, earlier[:, :, :], AX.X, ALU.add))
                    v.wait_ge(q["near"], i + 1)
                    v.wait_ge(q[f"feat{s}"], j * 16 + 16)
                    v.wait_ge(q["x_free"], i + 1)
                    own.did(v.tensor_tensor(xin[:, :, :], S.bank[s][0:TP, :].rearrange("p (t f) -> p t f", t=T),
                                            feat[:, s, :, :], ALU.add))
                    own.step(v.tensor_scalar(cnt, cnt, 1.0, None, ALU.min))
                    v.sem_inc(q["feat_free"], 1)
                    v.sem_inc(q["near_free"], 1)
                    v.sem_inc(q["x"], 1)
                    own.did(v.tensor_scalar(home[0:TP, 0, :], scol[0:TP, s, :], P - 1, None, ALU.bitwise_and))
                    own.step(v.tensor_scalar(home[0:TP, 1, :], scol[0:TP, s, :], 7, None, ALU.arith_shift_right))
                    own.step(v.scalar_tensor_tensor(home[0:TP, 2, :], home[0:TP, 0, :], float(NB), home[0:TP, 1, :], ALU.mult, ALU.add))
                    own.step(v.tensor_scalar(gap, home[0:TP, 2, :], -1.0, spare[0:TP, :], ALU.mult, ALU.add))
                    own.step(v.tensor_tensor(gap, gap, cnt, ALU.mult))
                    v.wait_ge(q["total_free"], i + 1)
                    own.step(v.tensor_tensor(to[0:TP, s, :], gap, home[0:TP, 2, :], ALU.add))
                    v.sem_inc(q["to"], 1)
                    v.sem_inc(q["cols_free"], 1)
                    assert own.n == STEPS, own.n

        @block.scalar
        def _(act):
            act.sem_inc(q["x_free"], 1)
            act.sem_inc(q["msg_free"], 2)
            with act.Fori(0, pairs_of(act)) as j:
                for s in range(2):
                    i = j * 2 + s
                    act.wait_ge(q["x"], i + 1)
                    act.wait_ge(q["sum_free"], i + 1)
                    for t in range(T):
                        op = nc.scalar.activation(msg[:, s, t, :], xin[:, t, :], ACT.Relu, scale=valid[:, s, t:t + 1])
                    op.then_inc(q["msg"], 1)
                    act.wait_ge(q["msg"], i + 1)
                    act.sem_inc(q["x_free"], 1)
                    act.sem_inc(q["msg_free"], 1)
                    act.wait_ge(q["sum"], i + 1)
                    act.wait_ge(q["total_free"], i + 1)
                    act.copy(total[0:TP, s, :, :], S.bank[2 + s][0:TP, :].rearrange("p (t f) -> p t f", t=T)).then_inc(q["total"], 1)

        @block.tensor
        def _(pe):
            pe.sem_inc(q["window_free"], 2)
            pe.sem_inc(q["same_free"], 2)
            pe.sem_inc(q["sum_free"], 2)
            with pe.Fori(0, pairs_of(pe)) as j:
                for s in range(2):
                    i = j * 2 + s
                    pe.wait_ge(q["there"], i + 1)
                    pe.wait_ge(q[f"hwin{s}"], j * 16 + 16)
                    pe.wait_ge(q["near_free"], i + 1)
                    for t in range(T):
                        mm = pe.matmul(S.bank[s][0:TP, t * D:(t + 1) * D],
                                       there[:, s, :].rearrange("k (p t) -> k t p", t=T)[:, t, :], hwin[:, s, :],
                                       start=True, stop=True, skip_group_check=True)
                    mm.then_inc(q["near"], 1)
                    pe.wait_ge(q["near"], i + 1)
                    pe.sem_inc(q["window_free"], 1)
                    pe.wait_ge(q["same"], i + 1)
                    pe.wait_ge(q["msg"], i + 1)
                    for t in range(T):
                        mm = pe.matmul(S.bank[2 + s][0:TP, t * D:(t + 1) * D], same[:, s, t, :], msg[:, s, t, :],
                                       start=True, stop=True, skip_group_check=True)
                    mm.then_inc(q["sum"], 1)
                    pe.wait_ge(q["sum"], i + 1)
                    pe.sem_inc(q["same_free"], 1)
                    pe.sem_inc(q["sum_free"], 1)


def mlp(nc, I, S, sb, sem):
    f3 = [P, NB, D]
    X, Hm = (sb(n, f3, F32)[:, :, :] for n in ("l_x", "l_h"))
    Y, tmp = (sb(n, [P, NB, 2 * D], F32)[:, :, :] for n in ("l_y", "l_tmp"))
    st = sb("l_st", [P, 4, NB], F32)[:, :, :]
    XT = sb("l_XT", [P, 2, P], F32)
    W1 = sb("l_w1", [D, 2 * D], F32)
    W2 = sb("l_w2", [2 * D, D], F32)
    rows = sb("l_rows", [P, 3, 2 * D], F32)
    b2 = sb("l_b2", [P, D], F32)
    eps = sb("l_eps", [P, 1], F32)
    fc = sb("l_fc", [D, D], F32)
    att = sb("l_att", [D, 2], F32)
    Wz = sb("l_wz", [D, D + 2], F32)
    esT = sb("l_esT", [NB, P], F32)
    accs = [Y[:, :, 0:D], Y[:, :, D:2 * D], tmp[:, :, 0:D], tmp[:, :, D:2 * D]]
    q = {n: sem("l_" + n) for n in ("x", "h", "acc", "acc1", "acc3", "w", "w3", "own", "var", "root", "in1", "in2", "in3", "store", "stored",
                                    "fct", "wz", "var2", "root2", "es", "est", "estc")}
    lins = [{n: sem(f"l_{n}{k}") for n in LINEAR} for k in range(3)]

    with nc.Block() as block:

        @block.sync
        def _(sp):
            by = "(b p) f -> p b f"
            flat = "(p b) f -> p b f"
            sp.dma_start(Hm, S.h2.rearrange(flat, p=P)).then_inc(q["h"], 16)
            sp.dma_start(eps[:, :], I["L2_gnn_eps"].unsqueeze(0).to_broadcast([P, 1])).then_inc(q["h"], 16)
            sp.dma_start(accs[0], S.acc[0][0:NP].rearrange(flat, p=P)).then_inc(q["acc"], 16)
            sp.dma_start(X, S.x2.rearrange(flat, p=P)).then_inc(q["x"], 16)
            sp.dma_start(W1[:, :], I["L2_gnn_W1"]).then_inc(q["w"], 16)
            sp.dma_start(W2[:, :], I["L2_gnn_W2"]).then_inc(q["w"], 16)
            for k, r in enumerate((I["L2_gnn_b1"], I["L2_gnn_ln_g"], I["L2_gnn_ln_b"])):
                sp.dma_start(rows[:, k, :], r.unsqueeze(0).to_broadcast([P, 2 * D])).then_inc(q["w"], 16)
            sp.dma_start(b2[:, :], I["L2_gnn_b2"].unsqueeze(0).to_broadcast([P, D])).then_inc(q["w"], 16)
            sp.dma_start(fc[:, :], I["L3_gnn_fc_w"]).then_inc(q["w3"], 16)
            with nc.allow_non_contiguous_dma(reason="128 values, once"):
                sp.dma_start(att[:, :], I["L3_gnn_attn_w"].rearrange("o (k c) -> c (o k)", k=2)).then_inc(q["w3"], 16)
            sp.wait_ge(q["store"], 1)
            sp.dma_start(S.x3.rearrange(by, p=P), X).then_inc(q["stored"], 16)
            sp.wait_ge(q["estc"], 1)
            sp.dma_start(S.z.rearrange(flat, p=P), Y[:, :, 0:D + 2]).then_inc(q["stored"], 16)
            sp.dma_start(S.es.rearrange("(b p) -> b p", p=P), esT[:, :]).then_inc(q["stored"], 16)
            sp.wait_ge(q["stored"], 48)

        @block.gpsimd
        def _(g):
            g.dma_start(accs[3], S.acc[3][0:NP].rearrange("(p b) f -> p b f", p=P)).then_inc(q["acc3"], 16)

        @block.tensor
        def _(pe):
            pe.wait_ge(q["w3"], 32)
            pe.transpose(S.bank[0][0:D, 0:D], fc[:, :], S.ident[0:D, 0:D])
            pe.matmul(S.bank[1][0:D, 0:2], fc[:, :], att[:, :], start=True, stop=True).then_inc(q["fct"], 1)
            pe.wait_ge(q["in1"], 1)
            pe.wait_ge(q["w"], 96)
            linear_pe(nc, S, lins[0], [Hm], XT, [W1[:, :]], 2 * D)
            pe.wait_ge(q["in2"], 1)
            linear_pe(nc, S, lins[1], [Y], XT, [W2[:, :]], D)
            pe.wait_ge(q["in3"], 1)
            pe.wait_ge(q["wz"], 2)
            linear_pe(nc, S, lins[2], [Hm], XT, [Wz[:, :]], D + 2)
            pe.wait_ge(q["es"], 1)
            pe.transpose(S.bank[0][0:NB, 0:P], Y[:, :, D], S.ident[:, :]).then_inc(q["est"], 1)

        @block.scalar
        def _(act):
            for a in (1, 2):
                act.dma_start(accs[a], S.acc[a][0:NP].rearrange("(p b) f -> p b f", p=P)).then_inc(q["acc1"], 16)
            act.wait_ge(q["fct"], 1)
            act.copy(Wz[:, 0:D], S.bank[0][0:D, 0:D]).then_inc(q["wz"], 1)
            act.copy(Wz[:, D:D + 2], S.bank[1][0:D, 0:2]).then_inc(q["wz"], 1)
            linear_act(nc, S, lins[0], 1, D, XT)
            act.wait_ge(q["var"], 1)
            root(nc, st, NB).then_inc(q["root"], 1)
            linear_act(nc, S, lins[1], 1, 2 * D, XT)
            act.wait_ge(q["var2"], 1)
            root(nc, st, NB).then_inc(q["root2"], 1)
            linear_act(nc, S, lins[2], 1, D, XT)
            act.wait_ge(q["est"], 1)
            act.copy(esT[:, :], S.bank[0][0:NB, 0:P]).then_inc(q["estc"], 1)

        @block.vector
        def _(v):
            own = Own(v, q["own"])
            v.wait_ge(q["h"], 32)
            v.wait_ge(q["acc"], 16)
            v.wait_ge(q["acc1"], 32)
            v.wait_ge(q["acc3"], 16)
            own.did(v.tensor_tensor(accs[0], accs[0], accs[1], ALU.add))
            own.step(v.tensor_tensor(accs[2], accs[2], accs[3], ALU.add))
            own.step(v.tensor_tensor(accs[0], accs[0], accs[2], ALU.add))
            own.step(v.scalar_tensor_tensor(accs[0], Hm, eps[:, :], accs[0], ALU.mult, ALU.add))
            own.step(v.tensor_tensor(Hm, Hm, accs[0], ALU.add))
            v.sem_inc(q["in1"], 1)
            v.wait_ge(q["w"], 96)
            for b in range(NB):
                v.wait_ge(lins[0]["lin"], b + 1)
                v.tensor_tensor(Y[:, b, :], S.bank[4 + b % 2][:, 0:2 * D], rows[:, 0, :], ALU.add).then_inc(lins[0]["lin_used"], 1)
            v.wait_ge(lins[0]["lin_used"], NB)

            def turn_of(var, done):
                def f():
                    v.sem_inc(q[var], 1)
                    v.wait_ge(q[done], 1)
                return f

            norm_steps(nc, own, Y, Y, tmp, st, 2 * D, False, turn_of("var", "root"))
            row = lambda k: rows[:, k, :].unsqueeze(1).to_broadcast([P, NB, 2 * D])
            own.step(v.tensor_tensor(tmp, tmp, row(1), ALU.mult))
            own.step(v.tensor_tensor(tmp, tmp, row(2), ALU.add))
            own.step(v.tensor_scalar(Y, tmp, 0.0, None, ALU.max))
            v.sem_inc(q["in2"], 1)
            v.wait_ge(q["x"], 16)
            own.step(v.tensor_tensor(X, X, b2[:, :].unsqueeze(1).to_broadcast(f3), ALU.add))
            for b in range(NB):
                v.wait_ge(lins[1]["lin"], b + 1)
                v.tensor_tensor(X[:, b, :], X[:, b, :], S.bank[4 + b % 2][:, 0:D], ALU.add).then_inc(lins[1]["lin_used"], 1)
            v.wait_ge(lins[1]["lin_used"], NB)
            v.sem_inc(q["store"], 1)
            norm_steps(nc, own, X, Hm, tmp[:, :, 0:D], st, D, True, turn_of("var2", "root2"))
            v.sem_inc(q["in3"], 1)
            for b in range(NB):
                v.wait_ge(lins[2]["lin"], b + 1)
                v.tensor_copy(Y[:, b, 0:D + 2], S.bank[4 + b % 2][:, 0:D + 2]).then_inc(lins[2]["lin_used"], 1)
            v.wait_ge(lins[2]["lin_used"], NB)
            v.sem_inc(q["es"], 1)


def gat(nc, I, S, sb, sem, out):
    CUT = [0, 7, 13, 19, NB]
    NC = len(CUT) - 1
    WIDE = 7 * P
    qrow = sb("g_q", [P, NP], F32)
    mask = sb("g_mask", [P, WIDE], F32)
    prob = sb("g_prob", [P, NC, WIDE], F32)
    Z = sb("g_z", [P, NB, D + 2], F32)
    low = sb("g_low", [P, 2, WIDE], F32)
    PT = sb("g_pt", [P, 3, 4 * P], F32)
    xb = sb("g_x", [P, D], F32)
    ob = sb("g_o", [P, D], F32)
    c = sb("g_c", [P, 16], F32)
    edc = sb("g_ed", [P, NB], F32)
    q = {n: sem("g_" + n) for n in (
        "z", "es", "own", "own2", "clip", "clip_free", "prob", "weigh", "top", "top_free", "high", "pt", "ptc", "pt_used",
        "num", "num_free", "x", "x_free", "ob", "ob_free", "out", "ready", "mid")}

    def size(k):
        return (CUT[k + 1] - CUT[k]) * P

    GR = -(-NB // 4)
    with nc.Block() as block:

        @block.sync
        def _(sp):
            sp.dma_start(qrow[:, :], S.es.unsqueeze(0).to_broadcast([P, NP])).then_inc(q["es"], 16)
            sp.dma_start(Z[:, :, :], S.z.rearrange("(p b) f -> p b f", p=P)).then_inc(q["z"], 16)
            with sp.Fori(0, NB - 1) as j:
                sp.wait_ge(q["x_free"], j + 1)
                sp.dma_start(xb[:, :], S.x3[bass.ds(j * P, P), :]).then_inc(q["x"], 16)
                sp.wait_ge(q["ob"], j + 1)
                sp.dma_start(out[bass.ds(j * P, P), :], ob[:, :]).then_inc(q["out"], 16)
                sp.wait_ge(q["out"], j * 16 + 16)
                sp.sem_inc(q["ob_free"], 1)
            sp.wait_ge(q["x_free"], NB)
            sp.dma_start(xb[:, :], S.x3[(NB - 1) * P:NP, :]).then_inc(q["x"], 16)
            sp.wait_ge(q["ob"], NB)
            sp.dma_start(out[(NB - 1) * P:N, :], ob[0:LAST, :]).then_inc(q["out"], 16)
            sp.wait_ge(q["out"], NB * 16)

        @block.vector
        def _(v):
            own = Own(v, q["own"])
            v.sem_inc(q["x_free"], 1)
            v.sem_inc(q["ob_free"], 1)
            v.sem_inc(q["num_free"], 1)
            v.sem_inc(q["high"], 2)
            v.wait_ge(q["es"], 16)
            own.step(v.tensor_reduce(c[:, 0:1], qrow[:, :], AX.X, ALU.min))
            own.step(v.tensor_scalar(c[:, 1:2], c[:, 0:1], -1.0, 1.0, ALU.mult, ALU.add))
            own.step(v.tensor_scalar(qrow[:, :], qrow[:, :], c[:, 1:2], None, ALU.add))
            v.wait_ge(q["z"], 16)
            own.step(v.tensor_scalar(edc[:, :], Z[:, :, D + 1], c[:, 1:2], None, ALU.subtract))
            own.step(v.memset(Z[:, :, D], 1.0))
            v.sem_inc(q["ready"], 1)
            BOUND, END = 2 * NC + 6, 4

            def greatest(mine, j, k):
                a, n = CUT[k] * P, size(k)
                mine.did(v.scalar_tensor_tensor(mask[:, 0:n], S.A[:, bass.ds(j * NP + a, n)], 1.0, qrow[:, a:a + n],
                                                ALU.min, ALU.mult))
                return lambda: mine.step(v.tensor_reduce(c[:, 4 + k:5 + k], mask[:, 0:n], AX.X, ALU.max))

            def clip(j, k):
                a, n = CUT[k] * P, size(k)
                v.wait_ge(q["clip_free"], j * NC + k + 1)
                v.tensor_scalar(prob[:, k, 0:n], qrow[:, a:a + n], c[:, 8:9], None, ALU.min).then_inc(q["clip"], 1)

            def bound(mine, j):
                v.wait_ge(q["top_free"], j + 1)
                mine.did(v.tensor_copy(c[:, 11:12], edc[:, bass.ds(j, 1)]))
                mine.step(v.tensor_reduce(c[:, 8:9], c[:, 4:4 + NC], AX.X, ALU.max))
                mine.step(v.tensor_tensor(c[:, 12:13], c[:, 8:9], c[:, 11:12], ALU.add))
                mine.step(v.scalar_tensor_tensor(c[:, 12:13], c[:, 12:13], 0.01, c[:, 12:13], ALU.mult, ALU.max))
                mine.did(v.tensor_tensor(c[:, 9:10], c[:, 11:12], c[:, 12:13], ALU.subtract))
                mine.step(v.scalar_tensor_tensor(c[:, 10:11], c[:, 11:12], 0.01, c[:, 12:13], ALU.mult, ALU.subtract))
                v.sem_inc(q["top"], 1)
                for k in range(NC - 1):
                    clip(j, k)

            def greater(j, k):
                n = size(k)
                v.wait_ge(q["prob"], j * NC + k + 1)
                v.tensor_tensor(prob[:, k, 0:n], prob[:, k, 0:n], low[:, k % 2, 0:n], ALU.max).then_inc(q["high"], 1)

            def finish(mine, j):
                v.wait_ge(q["num"], j + 1)
                num = S.bank[6]
                mine.step(v.tensor_scalar(c[:, 12:13], num[:, D:D + 1], 0.0, None, ALU.is_equal))
                mine.step(v.tensor_tensor(c[:, 13:14], num[:, D:D + 1], c[:, 12:13], ALU.add))
                mine.step(v.reciprocal(c[:, 14:15], c[:, 13:14]))
                v.wait_ge(q["x"], j * 16 + 16)
                v.wait_ge(q["ob_free"], j + 1)
                mine.step(v.scalar_tensor_tensor(ob[:, :], num[:, 0:D], c[:, 14:15], xb[:, :], ALU.mult, ALU.add))
                v.sem_inc(q["num_free"], 1)
                v.sem_inc(q["ob"], 1)
                v.sem_inc(q["x_free"], 1)

            mine = Own(v, q["own2"])
            for k in range(NC):
                reduced = greatest(mine, 0, k)
                mine.settle()
                reduced()
            bound(mine, 0)

            def weights(mine, j, last_block):
                for k in range(NC):
                    reduced = greatest(mine, j + 1, k)
                    if k == 0:
                        clip(j, NC - 1)
                    greater(j, k)
                    mine.settle()
                    reduced()
                    if k == 0 and last_block:
                        finish(mine, j - 1)
                bound(mine, j + 1)

            weights(mine, 0, False)
            with v.Fori(0, NB - 2) as j:
                mine = Own(v, q["own2"], j * (BOUND + END) + 2 * BOUND)
                weights(mine, j + 1, True)
                assert mine.n == BOUND + END
            mine = Own(v, q["own2"], NB * BOUND + (NB - 2) * END)
            clip(NB - 1, NC - 1)
            for k in range(NC):
                greater(NB - 1, k)
            finish(mine, NB - 2)
            finish(mine, NB - 1)

        @block.scalar
        def _(act):
            act.sem_inc(q["top_free"], 1)
            act.wait_ge(q["ready"], 1)

            def exponentials(j, k):
                n = size(k)
                if k == 0:
                    act.wait_ge(q["top"], j + 1)
                act.wait_ge(q["clip"], j * NC + k + 1)
                act.wait_ge(q["high"], j * NC + k + 1)
                nc.scalar.activation(low[:, k % 2, 0:n], prob[:, k, 0:n], ACT.Exp, bias=c[:, 10:11], scale=0.01).then_inc(q["mid"], 1)
                act.wait_ge(q["mid"], j * NC + k + 1)
                nc.scalar.activation(prob[:, k, 0:n], prob[:, k, 0:n], ACT.Exp, bias=c[:, 9:10]).then_inc(q["prob"], 1)

            def bring(j, n0, n1):
                for n in range(n0, n1):
                    act.wait_ge(q["pt"], j * GR + n + 1)
                    w = min(4, NB - 4 * n) * P
                    act.copy(PT[:, n % 3, 0:w], S.bank[n % 4][:, 0:w]).then_inc(q["ptc"], 1)

            def of_block(j, more):
                exponentials(j, 1)
                exponentials(j, 2)
                bring(j, 0, 1)
                exponentials(j, 3)
                bring(j, 1, 3)
                act.wait_ge(q["prob"], j * NC + NC)
                act.sem_inc(q["top_free"], 1)
                bring(j, 3, 4)
                if more:
                    exponentials(j + 1, 0)
                bring(j, 4, GR)

            assert NC == 4 and GR == 7
            exponentials(0, 0)
            with act.Fori(0, NB - 1) as j:
                of_block(j, True)
            of_block(NB - 1, False)

        @block.gpsimd
        def _(g):
            with g.Fori(0, NB) as j:
                for k in range(NC):
                    a, n = CUT[k] * P, size(k)
                    g.wait_ge(q["high"], j * NC + k + 3)
                    g.tensor_tensor(prob[:, k, 0:n], prob[:, k, 0:n], S.A[:, bass.ds(j * NP + a, n)], ALU.mult).then_inc(q["weigh"], 1)

        @block.tensor
        def _(pe):
            pe.sem_inc(q["clip_free"], NC)
            pe.wait_ge(q["ready"], 1)
            with pe.Fori(0, NB) as j:
                def products(n):
                    pe.wait_ge(q["ptc"], j * GR + n + 1)
                    if n == 0:
                        pe.wait_ge(q["num_free"], j + 1)
                    for b in range(4 * n, min(4 * n + 4, NB)):
                        mm = pe.matmul(S.bank[6][:, 0:D + 1], PT[:, n % 3, (b % 4) * P:(b % 4 + 1) * P], Z[:, b, 0:D + 1],
                                       start=(b == 0), stop=(b == NB - 1))
                    mm.then_inc(q["pt_used"], 1)

                for n in range(GR):
                    for b in range(4 * n, min(4 * n + 4, NB)):
                        k = max(x for x in range(NC) if CUT[x] <= b)
                        if b == CUT[k]:
                            pe.wait_ge(q["weigh"], j * NC + k + 1)
                        at = (b - CUT[k]) * P
                        mm = pe.transpose(S.bank[n % 4][:, (b % 4) * P:(b % 4 + 1) * P], prob[:, k, at:at + P], S.ident[:, :])
                    mm.then_inc(q["pt"], 1)
                    if n >= 2:
                        products(n - 2)
                    done = sum(CUT[k + 1] <= 4 * n + 4 for k in range(NC)) - sum(CUT[k + 1] <= 4 * n for k in range(NC))
                    if n == GR - 1:
                        done = 1
                    if done:
                        pe.wait_ge(q["pt"], j * GR + n + 1)
                        pe.sem_inc(q["clip_free"], done)
                products(GR - 2)
                products(GR - 1)
                pe.wait_ge(q["pt_used"], j * GR + GR)
                pe.sem_inc(q["num"], 1)


def build(nc, I, out):
    with ExitStack() as ctx:
        def sb_in(stack):
            return lambda name, shape, dt: stack.enter_context(nc.sbuf_tensor(name, shape, dt))

        taken = []

        def sem(name):
            taken.append(nc.alloc_semaphore(name))
            return taken[-1]

        def dram(name, shape, dt=F32):
            return nc.dram_tensor(name, shape, dt, kind="Internal").ap()

        keep = sb_in(ctx)
        S = Shared()
        S.A = keep("A", [P, NB * NP], BF16)
        S.ident = keep("ident", [P, P], F32)
        S.identb = keep("identb", [P, P], BF16)
        S.count = keep("count", [1, 3], I32)
        S.third = keep("third", [P, 1], I32)
        S.thirdf = keep("thirdf", [P, 1], F32)
        S.dinv = keep("dinv", [P, 3, NB], F32)
        S.ps = ctx.enter_context(nc.psum_tensor("ps", [P, 4096], F32))
        S.bank = [S.ps[:, 512 * k:512 * (k + 1)] for k in range(8)]
        S.items = dram("items", [P * IC, 2], I32)
        S.h0, S.xs, S.hs, S.x2, S.h2 = (dram(n, [NP, D]) for n in ("h0", "x1", "h1", "x2", "h2"))
        S.edges = dram("edge_table", [G, TP, 3, T])
        S.r3 = dram("r3", [NPW, SP3, H * D], BF16)
        S.h3 = dram("h3", [NPW, SP3, D], BF16)
        S.acc = [dram(f"acc{a}", [ACCR, D]) for a in range(NACC)]
        S.x3 = dram("x3", [NP, D])
        S.z = dram("z", [NP, D + 2])
        S.es = dram("es", [NP])

        with ExitStack() as layer0:
            more = sb_in(layer0)
            S.Mo = more("Mo", [D, H * D], F32)
            S.hpT = more("hpT", [D, NP], F32)
            S.ramp = more("ramp", [P, KEYS], I16)
            prepare(nc, I, S, sem)
            with ExitStack() as scratch:
                attend(nc, I, S, sb_in(scratch), sem)
            S.done = list(taken)
            with ExitStack() as scratch:
                turn(nc, I, S, sb_in(scratch), sem)
        with ExitStack() as scratch:
            chebyshev(nc, I, S, sb_in(scratch), sem)
        for stage in (messages, mlp):
            with ExitStack() as scratch:
                stage(nc, I, S, sb_in(scratch), sem)
        with ExitStack() as scratch:
            gat(nc, I, S, sb_in(scratch), sem, out)


_INS = ['x', 'src', 'dst', 'edge_attr_64', 'L0_gnn_Wq', 'L0_gnn_Wk', 'L0_gnn_Wv', 'L0_gnn_Wo', 'L0_gnn_gamma',
        'L0_gnn_beta', 'L1_gnn_W0', 'L1_gnn_b0', 'L1_gnn_W1', 'L1_gnn_b1', 'L2_gnn_W1', 'L2_gnn_b1', 'L2_gnn_ln_g',
        'L2_gnn_ln_b', 'L2_gnn_W2', 'L2_gnn_b2', 'L2_gnn_eps', 'L3_gnn_fc_w', 'L3_gnn_attn_w']


def kernel(**inputs):
    import numpy as _np
    import concourse.bacc as _bacc
    from concourse import mybir as _mybir
    from concourse.bass_utils import run_bass_kernel_spmd as _run

    nc = _bacc.Bacc("TRN2", target_bir_lowering=False, num_devices=1)
    arrays, args = {}, {}
    for name in _INS:
        a = _np.ascontiguousarray(inputs[name])
        arrays[f"in_{name}_dram"] = a
        args[name] = nc.dram_tensor(f"in_{name}_dram", a.shape, _mybir.dt.from_np(a.dtype), kind="ExternalInput").ap()
    out = nc.dram_tensor("out_0_dram", (3125, 64), _mybir.dt.float32, kind="ExternalOutput").ap()
    build(nc, args, out)
    r = _run(nc, [arrays], core_ids=[0])
    return r.results[0]["out_0_dram"]
```
